# Optimizing a Trainium2 kernel written in Bass

```python
import numpy as np
import jax
import jax.numpy as jnp

def _softmax(x, axis=-1):
    return jax.nn.softmax(x, axis=axis)

def _gelu(x):
    return jax.nn.gelu(x, approximate=True)

def _silu(x):
    return jax.nn.silu(x)

def _sigmoid(x):
    return jax.nn.sigmoid(x)

def _layernorm(x, axis=-1, eps=1e-05):
    m = jnp.mean(x, axis=axis, keepdims=True)
    v = jnp.var(x, axis=axis, keepdims=True)
    return (x - m) / jnp.sqrt(v + eps)

def _scatter_add(tgt, idx, src, axis=0):
    return tgt.at[idx].add(src)

def _segment_sum(src, seg, n):
    return jax.ops.segment_sum(src, seg, n)
kernel_name = 'mk_xattn_ffn_d1_seqx_r2_4e2d91'

def setup_inputs(seed: int=0):
    np.random.seed(seed)
    _w = jnp.asarray

    def _rec_inputs():
        import jax
        import jax.numpy as jnp
        _rk = jax.random.key(seed)
        x = -0.000125 + 0.9999 * jax.random.normal(jax.random.fold_in(_rk, 1), (8, 512, 2048), jnp.float32)
        _lenS = 512 - jax.random.randint(jax.random.fold_in(_rk, 7), (8,), 0, max(1, 512 // 4) + 1, jnp.int32)
        _lenS2 = 512 - jax.random.randint(jax.random.fold_in(_rk, 8), (8,), 0, max(1, 512 // 4) + 1, jnp.int32)
        _ctx_4096P = jax.random.normal(jax.random.fold_in(_rk, 11), (8, 16, 2048), jnp.float32)
        _ctx_4096c = jax.random.dirichlet(jax.random.fold_in(_rk, 511), 0.3 * jnp.ones((16,), jnp.float32), (8, 512))
        _ctx_4096t = jnp.einsum('bsk,bkd->bsd', _ctx_4096c, _ctx_4096P)
        _ctx_4096t = _ctx_4096t * jax.lax.rsqrt(jnp.mean(jnp.square(_ctx_4096t)) + 1e-12) * 0.953939
        ctx_4096 = -1.52775e-05 + 0.999936 * (_ctx_4096t + 0.3 * jax.random.normal(jax.random.fold_in(_rk, 611), (8, 512, 2048), jnp.float32))
        return (x, ctx_4096)
    x, ctx_4096 = _rec_inputs()

    def _L0_xattn_setup():
        import jax, jax.numpy as jnp
        import numpy as np
        B, C, D = (8, 512, 2048)
        GROUPS = 8
        ATTN_SCALE = 1.0
        RESID = 1.0
        EPS = 1e-05
        key = jax.random.key(seed)
        ks = jax.random.split(key, 9)
        s = 1.0 / np.sqrt(C)
        return {'inp_q': jax.random.normal(ks[0], (B, C, D), jnp.float32), 'inp_k': jax.random.normal(ks[1], (B, C, D), jnp.float32), 'inp_v': jax.random.normal(ks[2], (B, C, D), jnp.float32), 'Wt': jax.random.normal(ks[3], (C, C), jnp.float32) * s, 'Wp': jax.random.normal(ks[4], (C, C), jnp.float32) * s, 'Wg': jax.random.normal(ks[5], (C, C), jnp.float32) * s, 'Wz': jax.random.normal(ks[6], (C, C // GROUPS), jnp.float32) * s, 'gn_w': jax.random.normal(ks[7], (C,), jnp.float32), 'gn_b': jax.random.normal(ks[8], (C,), jnp.float32)}
    _L0_xattn_all = _L0_xattn_setup()
    _L0_xattn_in = {k: v for k, v in _L0_xattn_all.items() if k in ('Wt', 'Wp', 'Wg', 'Wz', 'gn_w', 'gn_b')}
    del _L0_xattn_all

    def _L0_ffn_setup():
        import jax, jax.numpy as jnp
        import numpy as np
        B, L, H, Dh, M = (4, 1024, 16, 128, 512)
        D = H * Dh
        key = jax.random.key(seed)
        kx, ku, kd, kp = jax.random.split(key, 4)
        x = jax.random.normal(kx, (B, L, D), dtype=jnp.float32)
        up = jax.random.normal(ku, (H, Dh, M), dtype=jnp.float32)
        down = jax.random.normal(kd, (H, M, Dh), dtype=jnp.float32)
        perm = jax.random.permutation(kp, D)
        return {'x': x, 'up': up, 'down': down, 'perm': perm}
    _L0_ffn_all = _L0_ffn_setup()
    _L0_ffn_in = {k: v for k, v in _L0_ffn_all.items() if k in ('up', 'down', 'perm')}
    del _L0_ffn_all
    return {'x': x, 'ctx_4096': ctx_4096, 'L0_xattn_Wt': _L0_xattn_in['Wt'], 'L0_xattn_Wp': _L0_xattn_in['Wp'], 'L0_xattn_Wg': _L0_xattn_in['Wg'], 'L0_xattn_Wz': _L0_xattn_in['Wz'], 'L0_xattn_gn_w': _L0_xattn_in['gn_w'], 'L0_xattn_gn_b': _L0_xattn_in['gn_b'], 'L0_ffn_up': _L0_ffn_in['up'], 'L0_ffn_down': _L0_ffn_in['down'], 'L0_ffn_perm': _L0_ffn_in['perm']}

def reference(x, ctx_4096, L0_xattn_Wt, L0_xattn_Wp, L0_xattn_Wg, L0_xattn_Wz, L0_xattn_gn_w, L0_xattn_gn_b, L0_ffn_up, L0_ffn_down, L0_ffn_perm):
    import jax
    import jax.numpy as jnp

    def _L0_xattn_ref(inp_q, inp_k, inp_v, Wt, Wp, Wg, Wz, gn_w, gn_b):
        import jax, jax.numpy as jnp
        import numpy as np
        B, C, D = (8, 512, 2048)
        GROUPS = 8
        ATTN_SCALE = 1.0
        RESID = 1.0
        EPS = 1e-05
        residual = inp_v * RESID
        t = jnp.einsum('oc,bcd->bod', Wt, inp_v)
        p = jnp.einsum('oc,bcd->bod', Wp, inp_q)
        g = jnp.einsum('oc,bcd->bod', Wg, inp_k)
        b, c, d = t.shape
        cg = c // GROUPS
        tg = t.reshape(b, GROUPS, cg * d)
        pg = p.reshape(b, GROUPS, cg * d)
        gg = g.reshape(b, GROUPS, cg * d)
        att = jnp.sum(pg * gg, axis=-1, keepdims=True) * ATTN_SCALE
        x = (att * tg).reshape(b, c, d)
        xg = x.reshape(b, GROUPS, cg, d)
        Wzg = Wz.reshape(GROUPS, cg, cg)
        y = jnp.einsum('goi,bgid->bgod', Wzg, xg).reshape(b, c, d)
        yg = y.reshape(b, GROUPS, cg * d)
        mu = jnp.mean(yg, axis=-1, keepdims=True)
        var = jnp.var(yg, axis=-1, keepdims=True)
        yn = ((yg - mu) * jax.lax.rsqrt(var + EPS)).reshape(b, c, d)
        return yn * gn_w[None, :, None] + gn_b[None, :, None] + residual

    def _L0_ffn_ref(x, up, down, perm):
        import jax, jax.numpy as jnp
        import numpy as np
        B, L, H, Dh, M = (4, 1024, 16, 128, 512)
        D = H * Dh
        b, l, Dm = x.shape
        h, d = (up.shape[0], up.shape[1])
        unperm = jnp.argsort(perm)
        t = x.reshape(b * l, Dm)
        t = t[:, perm]
        t = t.reshape(b * l, h, d)
        t = jnp.einsum('bhd,hdm->bhm', t, up)
        t = jax.nn.gelu(t, approximate=False)
        t = jnp.einsum('bhm,hmd->bhd', t, down)
        t = t.reshape(b * l, h * d)
        t = t[:, unperm]
        out = t.reshape(b, l, Dm)
        return out
    x = x + _L0_xattn_ref(_layernorm(x, axis=-1), ctx_4096, ctx_4096, L0_xattn_Wt, L0_xattn_Wp, L0_xattn_Wg, L0_xattn_Wz, L0_xattn_gn_w, L0_xattn_gn_b)
    x = x + _L0_ffn_ref(_layernorm(x, axis=-1), L0_ffn_up, L0_ffn_down, L0_ffn_perm)
    return x

_drawn_inputs = setup_inputs


def setup_inputs(seed=0):
    import zlib

    import numpy as np

    out = dict(_drawn_inputs(seed))
    spreads = {}
    factors = {'L0_xattn_gn_b': 8.0}
    for name, (base, spread) in spreads.items():
        noise = np.random.default_rng([zlib.crc32(name.encode()), seed]).standard_normal(out[name].shape)
        drawn = base * np.exp(spread * noise) if base else spread * noise
        out[name] = jnp.asarray(drawn.astype(out[name].dtype))
    for name, factor in factors.items():
        out[name] = (out[name] * factor).astype(out[name].dtype)
    return out
```

```python
from contextlib import ExitStack

import concourse.bass as bass
from concourse import mybir

F32 = mybir.dt.float32
F32R = mybir.dt.float32r
I32 = mybir.dt.int32
U32 = mybir.dt.uint32
ALU = mybir.AluOpType
ACT = mybir.ActivationFunctionType

B = 8
C = 512
D = 2048
P = 128
NT = C // P
W = 512
NQ = D // W
ND = D // P
M = 512
NM = M // P
EPS = 1e-5
LAG = 3
NC = 6


class Plan:

    def __init__(self, nc, ctx):
        self.nc, self.ctx = nc, ctx
        self.queue = {e: [] for e in ("pe", "act", "dve", "pool", "sp")}
        self.sems, self.count, self.seen = {}, {}, {}
        self.dma_sems = set()

    def sem(self, name):
        if name not in self.sems:
            self.sems[name] = self.ctx.enter_context(self.nc.semaphore("s_" + name))
            self.count[name] = 0
        return self.sems[name]

    def wait(self, e, *tokens):
        for t in tokens:
            if t is None:
                continue
            if isinstance(t, list):
                self.wait(e, *t)
                continue
            name, value = t
            if self.seen.get((e, name), 0) < value:
                self.seen[(e, name)] = value
                self.queue[e].append(lambda eng, s=self.sems[name], v=value: eng.wait_ge(s, v))

    def put(self, e, sem, make, waits=(), by=1):
        self.wait(e, *waits)
        s = self.sem(sem) if sem else None

        def run(eng):
            ins = make(eng)
            if s is not None:
                ins.then_inc(s, by)

        self.queue[e].append(run)
        if sem:
            self.count[sem] += by
            return (sem, self.count[sem])
        return None

    def dma(self, e, sem, out, in_, waits=()):
        self.dma_sems.add(sem)
        return self.put(e, sem, lambda eng: eng.dma_start(out, in_), waits, 16)


def build(nc, x, cx, Wt, WpT, Wg, WzT, gnw, gnb, up, down, perm, out):
    with ExitStack() as ctx:
        build_in(nc, ctx, x, cx, Wt, WpT, Wg, WzT, gnw, gnb, up, down, perm, out)


def build_in(nc, ctx, x, cx, Wt, WpT, Wg, WzT, gnw, gnb, up, down, perm, out):
    def sb(name, shape, dt=F32):
        return ctx.enter_context(nc.sbuf_tensor(name, shape, dt))

    def f(ap):
        return ap.bitcast(F32)

    pl = Plan(nc, ctx)
    put, dma, wait = pl.put, pl.dma, pl.wait

    bank = [ctx.enter_context(nc.psum_tensor(f"bank{k}", [P, 512], F32)) for k in range(8)]

    X = sb("X", [P, NT, D])
    Z = sb("Z", [P, NT, D])
    Ct = [sb(f"C{k}", [P, W]) for k in range(NC)]
    XL = [sb(f"XL{k}", [P, W]) for k in range(NT)]
    H8 = [sb(f"H{k}", [P, 512], F32R) for k in range(8)]
    T8 = [sb(f"T{k}", [P, 512], F32R) for k in range(8)]
    WCH = sb("WCH", [P, NT, C], F32R)
    WCL = sb("WCL", [P, NT, C], F32R)
    WP = sb("WP", [P, NT, C])
    WG = sb("WG", [P, NT, C])
    WR = sb("WR", [P, 2, 512])
    WH = [sb(f"WH{k}", [P, 2, 512], F32R) for k in range(2)]
    WL = [sb(f"WL{k}", [P, 2, 512], F32R) for k in range(2)]
    GR = [sb(f"GR{k}", [P, 512]) for k in range(3)]
    HR = [sb(f"HR{k}", [P, 512]) for k in range(3)]
    RB = sb("RB", [P, 4, 512])
    XR = [sb(f"XR{k}", [P, W]) for k in range(3)]
    OT = [sb(f"OT{k}", [P, 512]) for k in range(2)]
    XT = [sb(f"XT{k}", [P, 512]) for k in range(2)]
    ident = sb("ident", [P, P])
    avg = sb("avg", [P, P])
    perm_sb = sb("perm_sb", [P, ND], I32)
    gw = sb("gw", [P, NT])
    gb = sb("gb", [P, NT])
    half = sb("half", [P, NT])
    bn1 = sb("bn1", [P, NT, NQ * 6])
    bny = sb("bny", [P, NT, NQ * 6])
    bn2 = sb("bn2", [P, NT, NQ * 6])
    mv1 = sb("mv1", [P, NT, 2])
    mvy = sb("mvy", [P, NT, 2])
    mv2 = sb("mv2", [P, NT, 2])
    ve = sb("ve", [P, 3, NT])
    rs = sb("rs", [P, 3, NT])
    nm = sb("nm", [P, 2, NT])
    am = sb("am", [P, 2, NT])
    gm = sb("gm", [P, 2, NT])
    sm = sb("sm", [P, 6, NT])
    bc = sb("bc", [P, B, NT])


    ot_d = [nc.dram_tensor(f"ot_scratch{b}", [D, C], F32, kind="Internal") for b in range(B)]
    xg_d = [nc.dram_tensor(f"xg_scratch{b}", [D, C], F32, kind="Internal") for b in range(B)]
    x1_d = nc.dram_tensor("x1_scratch", [B, C, D], F32, kind="Internal")

    bank_free = [[] for _ in range(8)]
    C_free = [[] for _ in range(NC)]
    XL_free = [[] for _ in range(NT)]
    H8_free = [[] for _ in range(8)]
    T8_free = [[] for _ in range(8)]
    X_free = [[] for _ in range(NT)]
    Z_free = [[] for _ in range(NT)]
    WR_free, W_free = [], [[], []]
    GR_free = [[] for _ in range(3)]
    HR_free = [[] for _ in range(3)]
    RB_free = []
    XR_free = [[] for _ in range(3)]
    OT_free = [[] for _ in range(2)]
    XT_free = [[] for _ in range(2)]

    def setup():
        t = [dma("sp", "wt", Z[:, :, 0:C], Wt.rearrange("(t p) c -> p t c", p=P))]
        z = put("dve", "bd0", lambda e: e.memset(Z[:, 0, 1024:1536], 0.0))
        for g in range(2 * NT):
            h = g % 2
            t.append(dma("sp", f"wz{g}", Z[64 * h:64 * h + 64, 0, 1024 + 64 * g:1088 + 64 * g], WzT[g], [z]))
        s = {}
        s["wp"] = dma("sp", "wp", WP[:], WpT.rearrange("(t p) o -> p t o", p=P))
        s["wg"] = dma("sp", "wg", WG[:], Wg.rearrange("(t p) o -> p t o", p=P))
        s["perm"] = dma("sp", "perm", perm_sb[:], perm)
        s["gw"] = dma("sp", "gw", gw[:], gnw)
        s["gb"] = dma("sp", "gb", gb[:], gnb)
        z0 = put("pool", "id0", lambda e: e.memset(ident[:], 0.0))
        s["id"] = put("pool", "id", lambda e: e.affine_select(
            out=ident[:], in_=ident[:], compare_op=ALU.not_equal, fill=1.0, base=0,
            pattern=[[-1, P]], channel_multiplier=1), [z0])
        a0 = put("dve", "avg", lambda e: e.memset(avg[:], 0.0))
        put("dve", "avg", lambda e: e.memset(avg[0:64, 0:64], 1.0 / 64), [a0])
        s["avg"] = put("dve", "avg", lambda e: e.memset(avg[64:128, 64:128], 1.0 / 64))
        s["half"] = put("dve", "avg", lambda e: e.memset(half[:], -0.5))
        for ct in range(NT):
            wait("pe", t)
            for ot in range(NT):
                pe = put("pe", "wc" if ot == NT - 1 else None, lambda e, ct=ct, ot=ot: e.matmul(
                    bank[ct][:, ot * P:(ot + 1) * P], Z[:, ot, ct * P:(ct + 1) * P],
                    Z[:, 0, 1024 + ot * P:1024 + (ot + 1) * P], start=True, stop=True))
            a = put("act", "wch", lambda e, ct=ct: e.copy(WCH[:, ct, :], bank[ct][:]), [pe])
            s["wc"] = put("dve", "wcl", lambda e, ct=ct: e.tensor_tensor(
                WCL[:, ct, :], bank[ct][:], f(WCH[:, ct, :]), ALU.subtract), [a])
            s["wch"] = a
            bank_free[ct] = [s["wc"]]
        for ct in range(NT):
            Z_free[ct] = [pe]
        return s

    S = setup()
    state = {}

    def load_x(i, ct):
        state["x", i, ct] = dma("sp", f"x{ct}", X[:, ct, :], x[i, ct * P:(ct + 1) * P, :], X_free[ct])

    def bn_x(i, ct, q):
        state["bn1"] = put("dve", "bn1", lambda e: e.bn_stats(
            bn1[:, ct, 6 * q:6 * q + 6], X[:, ct, q * W:(q + 1) * W]), [state["x", i, ct], state.get("bn1free")])

    def norm(kind, bn, mv, last, free):
        k = {"1": 0, "2": 1}[kind]
        wait("dve", last, free)
        for ct in range(NT):
            t = put("dve", "mv" + kind, lambda e, ct=ct: e.bn_aggr(mv[:, ct, :], bn[:, ct, :]))
        state["bn" + kind + "free"] = t
        t1 = put("pool", "ve" + kind, lambda e: e.tensor_scalar(
            ve[:, k, :], mv[:, :, 1], EPS, None, ALU.add), [t])
        t2 = put("pool", "rs" + kind, lambda e: e.tensor_tensor(
            rs[:, k, :], ve[:, k, :], half[:], ALU.pow), [t1, S["half"]])
        t3 = put("dve", "nm" + kind, lambda e: e.scalar_tensor_tensor(
            out=nm[:, k, :], in0=mv[:, :, 0], scalar=-1.0, in1=rs[:, k, :], op0=ALU.mult, op1=ALU.mult), [t2])
        return [t2, t3]

    def norm_x(i):
        state["ln1", i] = norm("1", bn1, mv1, state["bn1"], state.get("xln"))

    cslot = {}
    nload = [0]

    def load_c(i, q, ct):
        if (i, q, ct) in cslot or i >= B:
            return
        k = nload[0] % NC
        nload[0] += 1
        cslot[i, q, ct] = k
        state["c", i, q, ct] = dma("sp", f"c{k}", Ct[k][:], cx[i, ct * P:(ct + 1) * P, q * W:(q + 1) * W], C_free[k])
        C_free[k] = []

    def xln(i, q):
        for ct in range(NT):
            t = put("act", "xln", lambda e, ct=ct: e.activation(
                XL[ct][:], X[:, ct, q * W:(q + 1) * W], ACT.Identity, bias=nm[:, 0, ct:ct + 1],
                scale=rs[:, 0, ct:ct + 1]), [state["x", i, ct], state["ln1", i], XL_free[ct]])
            XL_free[ct] = []
            state["xln", i, q, ct] = t
        state["xln"] = t

    def split_c(i, q, ct):
        k = cslot[i, q, ct]
        a = put("act", "chi", lambda e: e.copy(H8[ct][:], Ct[k][:]), [state["c", i, q, ct], H8_free[ct]])
        d = put("dve", "clo", lambda e: e.tensor_tensor(
            H8[4 + ct][:], Ct[k][:], f(H8[ct][:]), ALU.subtract), [a, H8_free[4 + ct]])
        state["cs", i, q, ct] = d
        C_free[k] += [a, d]

    def add_c(i, q, ct):
        k = cslot[i, q, ct]
        xs = X[:, ct, q * W:(q + 1) * W]
        d = put("dve", "xc", lambda e: e.tensor_tensor(xs, xs, Ct[k][:], ALU.add),
                [state["xln", i, q, ct], state["c", i, q, ct], state["bn1free"]])
        state["xc", i, q, ct] = d
        C_free[k] += [d]

    def turn(i, n):
        q, dt = divmod(n, 4)
        s = 4 * (n % 2)
        pe = []
        for w in range(2):
            bk = 4 + w
            wait("pe", bank_free[bk], S["id"])
            for ct in range(NT):
                k = cslot[i, q, ct]
                src = XL[ct] if w == 0 else Ct[k]
                need = state["xln", i, q, ct] if w == 0 else state["c", i, q, ct]
                t = put("pe", "tr" if ct == NT - 1 else None,
                        lambda e, bk=bk, ct=ct, src=src: e.transpose(
                            bank[bk][:, ct * P:(ct + 1) * P], src[:, dt * P:(dt + 1) * P], ident[:]), [need])
            pe.append(t)
        for ct in range(NT):
            if dt == 3:
                XL_free[ct] = [pe[0]]
                C_free[cslot[i, q, ct]] += [pe[1]]
        for w in range(2):
            h, l, bk = s + 2 * w, s + 2 * w + 1, 4 + w
            a = put("act", "thi", lambda e, h=h, bk=bk: e.copy(T8[h][:], bank[bk][:]), [pe[w], T8_free[h]])
            d = put("dve", "tlo", lambda e, h=h, l=l, bk=bk: e.tensor_tensor(
                T8[l][:], bank[bk][:], f(T8[h][:]), ALU.subtract), [a, T8_free[l]])
            bank_free[bk] = [d]
            state["ts", n, w] = [a, d]

    def s_mm(i, n):
        s = 4 * (n % 2)
        xh, xl, ch, cl = T8[s:s + 4]
        wait("pe", state["ts", n, 0], state["ts", n, 1])
        for c1 in range(NT):
            if n == 0:
                wait("pe", bank_free[c1])
            cs = slice(c1 * P, (c1 + 1) * P)
            for j, (a, b_) in enumerate(((xl, ch), (xh, cl), (xh, ch))):
                t = put("pe", "smm" if j == 2 else None, lambda e, a=a, b_=b_, j=j, c1=c1, cs=cs: e.matmul(
                    bank[c1][:], a[:, cs], b_[:], start=(n == 0 and j == 0), stop=(n == ND - 1 and j == 2)))
            state["smm", c1] = t
        for k in range(s, s + 4):
            T8_free[k] = [t]

    def y_mm(i, q, ot):
        bk = 6 + ot % 2
        os_ = slice(ot * P, (ot + 1) * P)
        wait("pe", bank_free[bk], S["wc"], S["wch"])
        for ct in range(NT):
            wait("pe", state["cs", i, q, ct])
            for j, (a, b_) in enumerate(((WCL, 0), (WCH, 4), (WCH, 0))):
                t = put("pe", "ymm" if (ct, j) == (NT - 1, 2) else None,
                        lambda e, a=a, b_=b_, j=j, ct=ct: e.matmul(
                            bank[bk][:], a[:, ct, os_], H8[b_ + ct][:],
                            start=(ct == 0 and j == 0), stop=(ct == NT - 1 and j == 2)))
        zs = Z[:, ot, q * W:(q + 1) * W]
        a = put("act", "yev", lambda e: e.copy(zs, bank[bk][:]), [t, Z_free[ot]])
        bank_free[bk] = [a]
        state["bny"] = put("dve", "bny", lambda e: e.bn_stats(bny[:, ot, 6 * q:6 * q + 6], zs),
                           [a, state.get("bnyfree")])
        state["y", i, q, ot] = a
        for k in range(8):
            H8_free[k] = [t]

    def s_out(i):
        for c1 in range(NT):
            a = put("act", "sev", lambda e, c1=c1: e.copy(XL[c1][:], bank[c1][:]), [state["smm", c1], XL_free[c1]])
            bank_free[c1] = [a]
            XL_free[c1] = []
            state["s", c1] = a

    nx = [0]

    def load_o(b, q):
        state["rb"] = dma("sp", "rb", RB[:], ot_d[b][q * W:(q + 1) * W, :].rearrange("(t p) c -> p t c", p=P),
                          [RB_free, state["scattered", b]])
        RB_free.clear()

    def load_xr(b, q, tt):
        k = nx[0] % 3
        nx[0] += 1
        state["xr", b, q, tt] = (k, dma("sp", f"xr{k}", XR[k][:], x1_d[b, tt * P:(tt + 1) * P, q * W:(q + 1) * W],
                                        [XR_free[k], state["x1st", b, tt]]))

    def out_unit(b, q, tt):
        bk = 6 + tt % 2
        wait("pe", bank_free[bk], state["rb"])
        for dt in range(4):
            t = put("pe", "otr" if dt == 3 else None, lambda e, dt=dt: e.transpose(
                bank[bk][:, dt * P:(dt + 1) * P], RB[:, dt, tt * P:(tt + 1) * P], ident[:]))
        RB_free[:] = [t]
        k, tok = state["xr", b, q, tt]
        d = put("dve", "fin", lambda e: e.scalar_tensor_tensor(
            out=XR[k][:], in0=bank[bk][:], scalar=bc[:, b, tt:tt + 1], in1=XR[k][:], op0=ALU.add, op1=ALU.add),
            [t, tok, state["bc", b]])
        bank_free[bk] = [d]
        XR_free[k] = [dma("pool", f"out{k}", out[b, tt * P:(tt + 1) * P, q * W:(q + 1) * W], XR[k][:], [d])]

    def aggr_y(i):
        for ot in range(NT):
            t = put("dve", "mvy", lambda e, ot=ot: e.bn_aggr(mvy[:, ot, :], bny[:, ot, :]),
                    [state["bny"], state.get("mvyfree")])
        state["bnyfree"] = t
        state["mvy"] = put("dve", "mvy", lambda e: e.tensor_copy(am[:, 1, :], mvy[:, :, 0]), [t, state.get("amfree")])

    def v_mm(i, ot):
        bk = ot % 2
        wait("pe", bank_free[bk], S["wp"], *[state["s", c1] for c1 in range(NT)])
        for c1 in range(NT):
            t = put("pe", "vmm" if c1 == NT - 1 else None, lambda e, c1=c1: e.matmul(
                bank[bk][:], WP[:, c1, ot * P:(ot + 1) * P], XL[c1][:], start=(c1 == 0), stop=(c1 == NT - 1)))
        d = put("dve", "att", lambda e: e.tensor_tensor_reduce(
            out=bank[bk][:], in0=bank[bk][:], in1=WG[:, ot, :], scale=1.0, scalar=0.0, op0=ALU.mult, op1=ALU.add,
            accum_out=am[:, 0, ot:ot + 1]), [t, S["wg"], state.get("amfree")])
        bank_free[bk] = [d]
        state["att", ot] = d
        for c1 in range(NT):
            XL_free[c1] = [t]

    def g_mean(i):
        t = put("pe", "gmm", lambda e: e.matmul(
            bank[0][:, 0:8], avg[:], am[:].rearrange("p a b -> p (a b)"), start=True, stop=True),
            [bank_free[0], S["avg"], state["mvy"], *[state["att", o] for o in range(NT)]])
        state["amfree"] = t
        c = put("dve", "gst", lambda e: e.tensor_copy(gm[:].rearrange("p a b -> p (a b)"), bank[0][:, 0:8]),
                [t])
        bank_free[0] = [c]
        d = put("dve", "gst", lambda e: e.tensor_tensor(sm[:, 0, :], am[:, 1, :], gm[:, 1, :], ALU.subtract), [c])
        d = put("dve", "gst", lambda e: e.tensor_tensor(sm[:, 1, :], sm[:, 0, :], sm[:, 0, :], ALU.mult), [d])
        state["sq"] = put("dve", "gst", lambda e: e.tensor_tensor(
            sm[:, 2, :], sm[:, 1, :], mvy[:, :, 1], ALU.add), [d])
        state["mvyfree"] = state["sq"]
        state["att"] = put("dve", "gst", lambda e: e.tensor_scalar(
            sm[:, 3, :], gm[:, 0, :], 64.0, None, ALU.mult), [c])

    def g_var(i):
        t = put("pe", "gmm", lambda e: e.matmul(bank[1][:, 0:4], avg[:], sm[:, 2, :], start=True, stop=True),
                [bank_free[1], state["sq"]])
        d = put("dve", "gst", lambda e: e.tensor_tensor(sm[:, 4, :], bank[1][:, 0:4], sm[:, 3, :], ALU.mult),
                [t, state["att"]])
        bank_free[1] = [d]
        d = put("dve", "gst", lambda e: e.tensor_tensor(sm[:, 4, :], sm[:, 4, :], sm[:, 3, :], ALU.mult), [d])
        p = put("pool", "gpw", lambda e: e.tensor_scalar(ve[:, 2, :], sm[:, 4, :], EPS, None, ALU.add), [d])
        p = put("pool", "gpw", lambda e: e.tensor_tensor(rs[:, 2, :], ve[:, 2, :], half[:], ALU.pow), [p])
        d = put("dve", "gst", lambda e: e.tensor_tensor(sm[:, 0, :], rs[:, 2, :], sm[:, 3, :], ALU.mult), [p])
        d = put("dve", "gst", lambda e: e.tensor_tensor(sm[:, 5, :], sm[:, 0, :], gw[:], ALU.mult),
                [d, S["gw"], state.get("x1")])
        state["A"] = d
        d = put("dve", "gst", lambda e: e.tensor_tensor(sm[:, 1, :], gm[:, 1, :], sm[:, 5, :], ALU.mult), [d])
        state["bc", i] = put("dve", "gst", lambda e: e.tensor_tensor(
            bc[:, i, :], gb[:], sm[:, 1, :], ALU.subtract), [d, S["gb"]])

    def x1_piece(i, ct, q):
        zs, xs = Z[:, ct, q * W:(q + 1) * W], X[:, ct, q * W:(q + 1) * W]
        d = put("dve", "x1", lambda e: e.scalar_tensor_tensor(
            out=zs, in0=zs, scalar=sm[:, 5, ct:ct + 1], in1=xs, op0=ALU.mult, op1=ALU.add),
            [state["A"], state["y", i, q, ct], state["xc", i, q, ct]])
        state["x1"] = d
        X_free[ct] = [d]
        state["bn2"] = put("dve", "bn2", lambda e: e.bn_stats(bn2[:, ct, 6 * q:6 * q + 6], zs),
                           [d, state.get("bn2free")])
        if q == NQ - 1:
            t = dma("pool", f"x1_{ct}", x1_d[i, ct * P:(ct + 1) * P, :], Z[:, ct, :], [d])
            state["x1st", i, ct] = t
            Z_free[ct] = [t]

    def norm_x1(i):
        state["ln2", i] = norm("2", bn2, mv2, state["bn2"], state.get("xln2"))

    def xln2(i, q):
        for ct in range(NT):
            t = put("act", "xln2", lambda e, ct=ct: e.activation(
                XL[ct][:], Z[:, ct, q * W:(q + 1) * W], ACT.Identity, bias=nm[:, 1, ct:ct + 1],
                scale=rs[:, 1, ct:ct + 1]), [state["ln2", i], state["x1"], XL_free[ct]])
            state["xln2", ct] = t
        state["xln2"] = t

    nxt = [0]

    def turn2(i, q, dt):
        bk, k = dt % 2, nxt[0] % 2
        nxt[0] += 1
        wait("pe", bank_free[bk])
        for ct in range(NT):
            t = put("pe", "tr2" if ct == NT - 1 else None, lambda e, ct=ct: e.transpose(
                bank[bk][:, ct * P:(ct + 1) * P], XL[ct][:, dt * P:(dt + 1) * P], ident[:]), [state["xln2", ct]])
        a = put("act", "xtv", lambda e: e.copy(XT[k][:], bank[bk][:]), [t, XT_free[k]])
        bank_free[bk] = [a]
        r = (4 * q + dt) * P
        XT_free[k] = [dma("sp", f"xt{k}", xg_d[i][r:r + P, :], XT[k][:], [a])]
        if dt == 3:
            for ct in range(NT):
                XL_free[ct] = [t]
            if q == NQ - 1:
                state["turned", i] = XT_free[0] + XT_free[1]

    def load_w(h):
        wait("sp", WR_free)
        dma("sp", "wr", WR[:, 0, :], up[h])
        state["wr"] = dma("sp", "wr", WR[:, 1, :].rearrange("p (t d) -> p t d", t=NM),
                          down[h].rearrange("(t p) d -> p t d", p=P))

    nw = [0]

    def split_w(h):
        k = nw[0] % 2
        nw[0] += 1
        a = put("act", "whi", lambda e: e.copy(WH[k][:], WR[:]), [state["wr"], W_free[k]])
        d = put("dve", "wlo", lambda e: e.tensor_tensor(WL[k][:], WR[:], f(WH[k][:]), ALU.subtract),
                [a, W_free[k]])
        WR_free[:] = [d]
        state["w"] = (k, [a, d])

    ng, ngs = [0], [0]

    def gather(b, h):
        k = ng[0] % 3
        ng[0] += 1
        pl.dma_sems.add(f"gr{k}")
        state["g", b, h] = (k, put("pool", f"gr{k}", lambda e: e.indirect_dma_start(
            out=GR[k][:], out_offset=None, in_=xg_d[b][:, :],
            in_offset=bass.IndirectOffsetOnAxis(ap=perm_sb[:, h:h + 1].bitcast(U32), axis=0)),
            [GR_free[k], state["turned", b], S["perm"]], 16))

    def split_g(b, h):
        k, tok = state["g", b, h]
        s = 2 * (ngs[0] % 2)
        ngs[0] += 1
        a = put("act", "ghi", lambda e: e.copy(T8[s][:], GR[k][:]), [tok, T8_free[s]])
        d = put("dve", "glo", lambda e: e.tensor_tensor(T8[s + 1][:], GR[k][:], f(T8[s][:]), ALU.subtract),
                [a, T8_free[s + 1]])
        GR_free[k] = [d]
        state["gs", b, h] = (s, [a, d])

    nu, nd, na = [0], [0], [0]

    def up_mm(b, h, mt, wk, wtok):
        u = nu[0]
        nu[0] += 1
        bk, r, hr = 4 + u % 4, u % 4, u % 3
        s, gtok = state["gs", b, h]
        wait("pe", bank_free[bk], gtok, wtok)
        ms = slice(mt * P, (mt + 1) * P)
        for j, (a, g) in enumerate(((WL[wk], T8[s]), (WH[wk], T8[s + 1]), (WH[wk], T8[s]))):
            t = put("pe", "up" if j == 2 else None, lambda e, a=a, g=g, j=j: e.matmul(
                bank[bk][:], a[:, 0, ms], g[:], start=(j == 0), stop=(j == 2)))
        if mt == NM - 1:
            T8_free[s] = [t]
            T8_free[s + 1] = [t]
        g = put("act", "gelu", lambda e: e.activation(HR[hr][:], bank[bk][:], ACT.Gelu), [t, HR_free[hr]])
        bank_free[bk] = [g]
        if u % 8 in HI_ACT:
            hi = put("act", "hhi", lambda e: e.copy(H8[r][:], HR[hr][:]), [g, H8_free[r]])
        else:
            hi = put("dve", "hhd", lambda e: e.tensor_copy(H8[r][:], HR[hr][:]), [g, H8_free[r]])
        lo = put("dve", "hlo", lambda e: e.tensor_tensor(H8[4 + r][:], HR[hr][:], f(H8[r][:]), ALU.subtract),
                 [g, hi, H8_free[4 + r]])
        HR_free[hr] = [hi, lo]
        return (b, h, mt, wk, r, [hi, lo])

    def down_mm(b, h, mt, wk, r, htok):
        if mt == 0:
            na[0] += 1
        bk, k = 2 + na[0] % 2, na[0] % 2
        if mt == 0:
            wait("pe", bank_free[bk])
        wait("pe", htok)
        ms = slice(mt * P, (mt + 1) * P)
        for j, (a, hh) in enumerate(((WL[wk], H8[r]), (WH[wk], H8[4 + r]), (WH[wk], H8[r]))):
            t = put("pe", "dn" if j == 2 else None, lambda e, a=a, hh=hh, j=j: e.matmul(
                bank[bk][:], a[:, 1, ms], hh[:], start=(mt == 0 and j == 0), stop=(mt == NM - 1 and j == 2)))
        H8_free[r] = [t]
        H8_free[4 + r] = [t]
        W_free[wk] = [t]
        if mt == NM - 1:
            a = put("act", "oev", lambda e: e.copy(OT[k][:], bank[bk][:]), [t, OT_free[k]])
            bank_free[bk] = [a]
            pl.dma_sems.add(f"sc{k}")
            OT_free[k] = [put("pool", f"sc{k}", lambda e: e.indirect_dma_start(
                out=ot_d[b][:, :], out_offset=bass.IndirectOffsetOnAxis(
                    ap=perm_sb[:, h:h + 1].bitcast(U32), axis=0),
                in_=OT[k][:], in_offset=None), [a, S["perm"]], 16)]
            if h == ND - 1:
                state["scattered", b] = OT_free[0] + OT_free[1]

    HI_ACT = (0, 2, 4)

    def phase_gs(p):
        if not 0 <= p < B:
            return []
        return [(b, h) for h in range(8 * (p % 2), 8 * (p % 2) + 8) for b in (p // 2 * 2, p // 2 * 2 + 1)]

    def p1_start(i):
        xln(i, 0)
        for ct in range(NT):
            load_c(i, 0, ct)

    def o_load(b, q):
        if 0 <= b < B:
            load_o(b, q)
            for tt in range(3):
                load_xr(b, q, tt)

    def p1(i):
        if i < B:
            turn(i, 0)
        b = i - 4
        gs = phase_gs(i - 2)
        if b >= 0:
            o_load(b, 0)
        for q in range(NQ):
            for s in range(4):
                n = 4 * q + s
                if i < B:
                    if n + 1 < ND:
                        turn(i, n + 1)
                    s_mm(i, n)
                    if s == 0:
                        for ct in range(NT):
                            split_c(i, q, ct)
                    if s == 1:
                        for ct in range(NT):
                            add_c(i, q, ct)
                    if s == 2:
                        for ct in range(NT):
                            nxt_q, nxt_i = (q + 1, i) if q + 1 < NQ else (0, i + 1)
                            if not (nxt_i != i and ct >= 2):
                                load_c(nxt_i, nxt_q, ct)
                        if q + 1 < NQ:
                            xln(i, q + 1)
                if s < 2 and b >= 0:
                    for tt in (2 * s, 2 * s + 1):
                        out_unit(b, q, tt)
                        if tt == 0:
                            load_xr(b, q, 3)
                if s == 2 and b >= 0 and q + 1 < NQ:
                    o_load(b, q + 1)
                if q == NQ - 1 and gs:
                    if s == 0:
                        load_w(gs[0][1])
                        gather(*gs[0])
                        gather(*gs[1])
                    if s == 1:
                        split_w(gs[0][1])
                    if s == 3:
                        split_g(*gs[0])
                        gather(*gs[2])
                if i < B:
                    if n == ND - 1:
                        s_out(i)
                    if s >= 2:
                        y_mm(i, q, 2 * (s - 2))
                        y_mm(i, q, 2 * (s - 2) + 1)

    def side_tasks(i):
        r = []
        if i < B:
            r.append((1, lambda: aggr_y(i)))
            for ot in range(NT):
                r.append((2 + 2 * ot, lambda ot=ot: v_mm(i, ot)))
            r.append((10, lambda: g_mean(i)))
            r.append((12, lambda: g_var(i)))
            for k in range(16):
                ct, q = divmod(k, 4)
                r.append((13 + 2 * k, lambda ct=ct, q=q: x1_piece(i, ct, q)))
                if q == 3 and i + 1 < B:
                    r.append((14 + 2 * k, lambda ct=ct: load_x(i + 1, ct)))
            r.append((45, lambda: norm_x1(i)))
            for q in range(NQ):
                r.append((46 + 4 * q, lambda q=q: xln2(i, q)))
                for dt in range(4):
                    r.append((46 + 4 * q + dt + (1 if q < 3 else 0) * 1, lambda q=q, dt=dt: turn2(i, q, dt)))
            if i + 1 < B:
                for k in range(16):
                    ct, q = divmod(k, 4)
                    r.append((29 + 2 * k + 1, lambda ct=ct, q=q: bn_x(i + 1, ct, q)))
                r.append((63, lambda: norm_x(i + 1)))
        return sorted(r, key=lambda t: t[0])

    def fslot(i):
        tasks = side_tasks(i)
        gs = phase_gs(i - 2)
        wk = None
        pend = []
        for g, (b, h) in enumerate(gs):
            if g % 2 == 0:
                wk, wtok = state["w"]
            for mt in range(NM):
                u = 4 * g + mt
                while tasks and tasks[0][0] <= u:
                    tasks.pop(0)[1]()
                up_t = up_mm(b, h, mt, wk, wtok)
                pend.append(up_t)
                if mt == 0 and g % 2 == 0 and g + 2 < len(gs):
                    load_w(gs[g + 2][1])
                if mt == 1 and g + 1 < len(gs):
                    split_g(*gs[g + 1])
                    if g + 3 < len(gs):
                        gather(*gs[g + 3])
                if len(pend) > LAG:
                    down_mm(*pend.pop(0))
                if mt == 2 and g % 2 == 1 and g + 1 < len(gs):
                    split_w(gs[g + 1][1])
        for _, t in tasks:
            t()
        if i + 1 < B:
            p1_start(i + 1)
        for a in pend:
            down_mm(*a)

    for ct in range(NT):
        load_x(0, ct)
    for ct in range(NT):
        load_c(0, 0, ct)
    for ct in range(NT):
        for q in range(NQ):
            bn_x(0, ct, q)
    norm_x(0)
    p1_start(0)
    for i in range(B + 4):
        p1(i)
        if i < B + 2:
            fslot(i)

    for name in sorted(pl.dma_sems):
        wait("sp", (name, pl.count[name]))

    block = ctx.enter_context(nc.Block())

    def run(name, eng):
        for fn in pl.queue[name]:
            fn(eng)

    @block.sync
    def _(e):
        run("sp", e)

    @block.tensor
    def _(e):
        run("pe", e)

    @block.scalar
    def _(e):
        run("act", e)

    @block.vector
    def _(e):
        run("dve", e)

    @block.gpsimd
    def _(e):
        run("pool", e)


def kernel(x, ctx_4096, L0_xattn_Wt, L0_xattn_Wp, L0_xattn_Wg, L0_xattn_Wz, L0_xattn_gn_w, L0_xattn_gn_b,
           L0_ffn_up, L0_ffn_down, L0_ffn_perm):
    import numpy as np
    import concourse.bacc as bacc
    from concourse.bass_utils import run_bass_kernel_spmd

    ins = {
        "x": x, "cx": ctx_4096, "Wt": L0_xattn_Wt, "WpT": np.asarray(L0_xattn_Wp).T, "Wg": L0_xattn_Wg,
        "WzT": np.asarray(L0_xattn_Wz).reshape(8, 64, 64).transpose(0, 2, 1),
        "gnw": np.asarray(L0_xattn_gn_w).reshape(4, 128).T, "gnb": np.asarray(L0_xattn_gn_b).reshape(4, 128).T,
        "up": L0_ffn_up, "down": L0_ffn_down, "perm": np.asarray(L0_ffn_perm).reshape(16, 128).T,
    }
    nc = bacc.Bacc("TRN2", target_bir_lowering=False, num_devices=1)
    arrays, args = {}, []
    for name, a in ins.items():
        a = np.ascontiguousarray(a)
        arrays["in_" + name] = a
        args.append(nc.dram_tensor("in_" + name, a.shape, mybir.dt.from_np(a.dtype), kind="ExternalInput").ap())
    args.append(nc.dram_tensor("out_0", (8, 512, 2048), F32, kind="ExternalOutput").ap())
    build(nc, *args)
    r = run_bass_kernel_spmd(nc, [arrays], core_ids=[0])
    return r.results[0]["out_0"]
```

```python
from contextlib import ExitStack

import concourse.bass as bass
from concourse import mybir

F32 = mybir.dt.float32
F32R = mybir.dt.float32r
I32 = mybir.dt.int32
U32 = mybir.dt.uint32
ALU = mybir.AluOpType
ACT = mybir.ActivationFunctionType

B = 8
C = 512
D = 2048
P = 128
NT = C // P
W = 512
NQ = D // W
ND = D // P
M = 512
NM = M // P
EPS = 1e-5
LAG = 3
NC = 6


class Plan:

    def __init__(self, nc, ctx):
        self.nc, self.ctx = nc, ctx
        self.queue = {e: [] for e in ("pe", "act", "dve", "pool", "sp")}
        self.sems, self.count, self.seen = {}, {}, {}
        self.dma_sems = set()

    def sem(self, name):
        if name not in self.sems:
            self.sems[name] = self.ctx.enter_context(self.nc.semaphore("s_" + name))
            self.count[name] = 0
        return self.sems[name]

    def wait(self, e, *tokens):
        for t in tokens:
            if t is None:
                continue
            if isinstance(t, list):
                self.wait(e, *t)
                continue
            name, value = t
            if self.seen.get((e, name), 0) < value:
                self.seen[(e, name)] = value
                self.queue[e].append(lambda eng, s=self.sems[name], v=value: eng.wait_ge(s, v))

    def put(self, e, sem, make, waits=(), by=1):
        self.wait(e, *waits)
        s = self.sem(sem) if sem else None

        def run(eng):
            ins = make(eng)
            if s is not None:
                ins.then_inc(s, by)

        self.queue[e].append(run)
        if sem:
            self.count[sem] += by
            return (sem, self.count[sem])
        return None

    def dma(self, e, sem, out, in_, waits=()):
        self.dma_sems.add(sem)
        return self.put(e, sem, lambda eng: eng.dma_start(out, in_), waits, 16)


def build(nc, x, cx, Wt, WpT, Wg, WzT, gnw, gnb, up, down, perm, out):
    with ExitStack() as ctx:
        build_in(nc, ctx, x, cx, Wt, WpT, Wg, WzT, gnw, gnb, up, down, perm, out)


def build_in(nc, ctx, x, cx, Wt, WpT, Wg, WzT, gnw, gnb, up, down, perm, out):
    def sb(name, shape, dt=F32):
        return ctx.enter_context(nc.sbuf_tensor(name, shape, dt))

    def f(ap):
        return ap.bitcast(F32)

    pl = Plan(nc, ctx)
    put, dma, wait = pl.put, pl.dma, pl.wait

    bank = [ctx.enter_context(nc.psum_tensor(f"bank{k}", [P, 512], F32)) for k in range(8)]

    X = sb("X", [P, NT, D])
    Z = sb("Z", [P, NT, D])
    Ct = [sb(f"C{k}", [P, W]) for k in range(NC)]
    XL = [sb(f"XL{k}", [P, W]) for k in range(NT)]
    H8 = [sb(f"H{k}", [P, 512], F32R) for k in range(8)]
    T8 = [sb(f"T{k}", [P, 512], F32R) for k in range(8)]
    WCH = sb("WCH", [P, NT, C], F32R)
    WCL = sb("WCL", [P, NT, C], F32R)
    WP = sb("WP", [P, NT, C])
    WG = sb("WG", [P, NT, C])
    WR = sb("WR", [P, 2, 512])
    WH = [sb(f"WH{k}", [P, 2, 512], F32R) for k in range(2)]
    WL = [sb(f"WL{k}", [P, 2, 512], F32R) for k in range(2)]
    GR = [sb(f"GR{k}", [P, 512]) for k in range(3)]
    HR = [sb(f"HR{k}", [P, 512]) for k in range(3)]
    RB = sb("RB", [P, 4, 512])
    XR = [sb(f"XR{k}", [P, W]) for k in range(3)]
    OT = [sb(f"OT{k}", [P, 512]) for k in range(2)]
    XT = [sb(f"XT{k}", [P, 512]) for k in range(2)]
    ident = sb("ident", [P, P])
    avg = sb("avg", [P, P])
    perm_sb = sb("perm_sb", [P, ND], I32)
    gw = sb("gw", [P, NT])
    gb = sb("gb", [P, NT])
    half = sb("half", [P, NT])
    bn1 = sb("bn1", [P, NT, NQ * 6])
    bny = sb("bny", [P, NT, NQ * 6])
    bn2 = sb("bn2", [P, NT, NQ * 6])
    mv1 = sb("mv1", [P, NT, 2])
    mvy = sb("mvy", [P, NT, 2])
    mv2 = sb("mv2", [P, NT, 2])
    ve = sb("ve", [P, 3, NT])
    rs = sb("rs", [P, 3, NT])
    nm = sb("nm", [P, 2, NT])
    am = sb("am", [P, 2, NT])
    gm = sb("gm", [P, 2, NT])
    sm = sb("sm", [P, 6, NT])
    bc = sb("bc", [P, B, NT])


    ot_d = [nc.dram_tensor(f"ot_scratch{b}", [D, C], F32, kind="Internal") for b in range(B)]
    xg_d = [nc.dram_tensor(f"xg_scratch{b}", [D, C], F32, kind="Internal") for b in range(B)]
    x1_d = nc.dram_tensor("x1_scratch", [B, C, D], F32, kind="Internal")

    bank_free = [[] for _ in range(8)]
    C_free = [[] for _ in range(NC)]
    XL_free = [[] for _ in range(NT)]
    H8_free = [[] for _ in range(8)]
    T8_free = [[] for _ in range(8)]
    X_free = [[] for _ in range(NT)]
    Z_free = [[] for _ in range(NT)]
    WR_free, W_free = [[], []], [[[], []], [[], []]]
    GR_free = [[] for _ in range(3)]
    HR_free = [[] for _ in range(3)]
    RB_free = []
    XR_free = [[] for _ in range(3)]
    OT_free = [[] for _ in range(2)]
    XT_free = [[] for _ in range(2)]

    S = {}

    def setup():
        z = put("dve", "bd0", lambda e: e.memset(Z[:, 0, 1024:1536], 0.0))
        S["wt"] = [dma("sp", "wt", Z[:, :, 0:C], Wt.rearrange("(t p) c -> p t c", p=P))]
        for g in range(2 * NT):
            h = g % 2
            S["wt"].append(dma("sp", f"wz{g}", Z[64 * h:64 * h + 64, 0, 1024 + 64 * g:1088 + 64 * g], WzT[g], [z]))
        S["wp"] = dma("sp", "wp", WP[:], WpT.rearrange("(t p) o -> p t o", p=P))
        S["wg"] = dma("sp", "wg", WG[:], Wg.rearrange("(t p) o -> p t o", p=P))
        S["perm"] = dma("sp", "perm", perm_sb[:], perm)
        S["gw"] = dma("sp", "gw", gw[:], gnw)
        S["gb"] = dma("sp", "gb", gb[:], gnb)

    def constants():
        S["half"] = put("dve", "half", lambda e: e.memset(half[:], -0.5))
        z0 = put("pool", "id0", lambda e: e.memset(ident[:], 0.0))
        S["id"] = put("pool", "id", lambda e: e.affine_select(
            out=ident[:], in_=ident[:], compare_op=ALU.not_equal, fill=1.0, base=0,
            pattern=[[-1, P]], channel_multiplier=1), [z0])
        a0 = put("dve", "avg", lambda e: e.memset(avg[:], 0.0))
        put("dve", "avg", lambda e: e.memset(avg[0:64, 0:64], 1.0 / 64), [a0])
        S["avg"] = put("dve", "avg", lambda e: e.memset(avg[64:128, 64:128], 1.0 / 64))

    def fold():
        wait("pe", S["wt"])
        for ct in range(NT):
            bk = 6 + ct % 2
            wait("pe", bank_free[bk])
            for ot in range(NT):
                pe = put("pe", "wc" if ot == NT - 1 else None, lambda e, bk=bk, ct=ct, ot=ot: e.matmul(
                    bank[bk][:, ot * P:(ot + 1) * P], Z[:, ot, ct * P:(ct + 1) * P],
                    Z[:, 0, 1024 + ot * P:1024 + (ot + 1) * P], start=True, stop=True))
            a = put("act", "wch", lambda e, bk=bk, ct=ct: e.copy(WCH[:, ct, :], bank[bk][:]), [pe])
            S["wc"] = put("dve", "wcl", lambda e, bk=bk, ct=ct: e.tensor_tensor(
                WCL[:, ct, :], bank[bk][:], f(WCH[:, ct, :]), ALU.subtract), [a])
            S["wch"] = a
            bank_free[bk] = [S["wc"]]
        for ct in range(NT):
            Z_free[ct] = [pe]

    state = {}

    def load_x(i, ct):
        state["x", i, ct] = dma("sp", f"x{ct}", X[:, ct, :], x[i, ct * P:(ct + 1) * P, :], X_free[ct])

    def bn_x(i, ct, q):
        state["bn1", ct] = put("dve", "bn1", lambda e: e.bn_stats(
            bn1[:, ct, 6 * q:6 * q + 6], X[:, ct, q * W:(q + 1) * W]), [state["x", i, ct]])

    def norm_a(kind, ct, bn, mv, last, free):
        k = {"1": 0, "2": 1}[kind]
        t = put("dve", "mv" + kind, lambda e: e.bn_aggr(mv[:, ct, :], bn[:, ct, :]), [last, free])
        t1 = put("pool", "ve" + kind, lambda e: e.tensor_scalar(
            ve[:, k, ct:ct + 1], mv[:, ct, 1:2], EPS, None, ALU.add), [t])
        return put("pool", "rs" + kind, lambda e: e.tensor_tensor(
            rs[:, k, ct:ct + 1], ve[:, k, ct:ct + 1], half[:, 0:1], ALU.pow), [t1, S["half"]])

    def norm_b(kind, ct, mv, t2):
        k = {"1": 0, "2": 1}[kind]
        t3 = put("dve", "nm" + kind, lambda e: e.scalar_tensor_tensor(
            out=nm[:, k, ct:ct + 1], in0=mv[:, ct, 0:1], scalar=-1.0, in1=rs[:, k, ct:ct + 1],
            op0=ALU.mult, op1=ALU.mult), [t2])
        return [t2, t3]

    def norm_x_a(i, ct):
        state["n1", ct] = norm_a("1", ct, bn1, mv1, state["bn1", ct], state.get(("xln", ct)))

    def norm_x_b(i, ct):
        state["ln1", i, ct] = norm_b("1", ct, mv1, state["n1", ct])

    cslot = {}
    nload = [0]

    def load_c(i, q, ct):
        if (i, q, ct) in cslot or i >= B:
            return
        k = nload[0] % NC
        nload[0] += 1
        cslot[i, q, ct] = k
        state["c", i, q, ct] = dma("sp", f"c{k}", Ct[k][:], cx[i, ct * P:(ct + 1) * P, q * W:(q + 1) * W], C_free[k])
        C_free[k] = []

    def xln(i, q):
        for ct in range(NT):
            t = put("act", "xln", lambda e, ct=ct: e.activation(
                XL[ct][:], X[:, ct, q * W:(q + 1) * W], ACT.Identity, bias=nm[:, 0, ct:ct + 1],
                scale=rs[:, 0, ct:ct + 1]), [state["x", i, ct], state["ln1", i, ct], XL_free[ct]])
            XL_free[ct] = []
            state["xln", i, q, ct] = t
            state["xln", ct] = t

    def split_c(i, q, ct):
        k = cslot[i, q, ct]
        a = put("act", "chi", lambda e: e.copy(H8[ct][:], Ct[k][:]), [state["c", i, q, ct], H8_free[ct]])
        d = put("dve", "clo", lambda e: e.tensor_tensor(
            H8[4 + ct][:], Ct[k][:], f(H8[ct][:]), ALU.subtract), [a, H8_free[4 + ct]])
        state["cs", i, q, ct] = d
        C_free[k] += [a, d]

    def add_c(i, q, ct):
        k = cslot[i, q, ct]
        xs = X[:, ct, q * W:(q + 1) * W]
        d = put("dve", "xc", lambda e: e.tensor_tensor(xs, xs, Ct[k][:], ALU.add),
                [state["xln", i, q, ct], state["c", i, q, ct], state["bn1", ct]])
        state["xc", i, q, ct] = d
        C_free[k] += [d]

    def turn(i, n):
        q, dt = divmod(n, 4)
        s = 4 * (n % 2)
        pe = []
        for w in range(2):
            bk = 4 + w
            wait("pe", bank_free[bk], S["id"])
            for ct in range(NT):
                k = cslot[i, q, ct]
                src = XL[ct] if w == 0 else Ct[k]
                need = state["xln", i, q, ct] if w == 0 else state["c", i, q, ct]
                t = put("pe", "tr" if ct == NT - 1 else None,
                        lambda e, bk=bk, ct=ct, src=src: e.transpose(
                            bank[bk][:, ct * P:(ct + 1) * P], src[:, dt * P:(dt + 1) * P], ident[:]), [need])
            pe.append(t)
        for ct in range(NT):
            if dt == 3:
                XL_free[ct] = [pe[0]]
                C_free[cslot[i, q, ct]] += [pe[1]]
        for w in range(2):
            h, l, bk = s + 2 * w, s + 2 * w + 1, 4 + w
            a = put("act", "thi", lambda e, h=h, bk=bk: e.copy(T8[h][:], bank[bk][:]), [pe[w], T8_free[h]])
            d = put("dve", "tlo", lambda e, h=h, l=l, bk=bk: e.tensor_tensor(
                T8[l][:], bank[bk][:], f(T8[h][:]), ALU.subtract), [a, T8_free[l]])
            bank_free[bk] = [d]
            state["ts", n, w] = [a, d]

    def s_mm(i, n):
        s = 4 * (n % 2)
        xh, xl, ch, cl = T8[s:s + 4]
        wait("pe", state["ts", n, 0], state["ts", n, 1])
        for c1 in range(NT):
            if n == 0:
                wait("pe", bank_free[c1])
            cs = slice(c1 * P, (c1 + 1) * P)
            for j, (a, b_) in enumerate(((xl, ch), (xh, cl), (xh, ch))):
                t = put("pe", "smm" if j == 2 else None, lambda e, a=a, b_=b_, j=j, c1=c1, cs=cs: e.matmul(
                    bank[c1][:], a[:, cs], b_[:], start=(n == 0 and j == 0), stop=(n == ND - 1 and j == 2)))
            state["smm", c1] = t
        for k in range(s, s + 4):
            T8_free[k] = [t]

    def y_mm(i, q, ot):
        bk = 6 + ot % 2
        os_ = slice(ot * P, (ot + 1) * P)
        wait("pe", bank_free[bk], S["wc"], S["wch"])
        for ct in range(NT):
            wait("pe", state["cs", i, q, ct])
            for j, (a, b_) in enumerate(((WCL, 0), (WCH, 4), (WCH, 0))):
                t = put("pe", "ymm" if (ct, j) == (NT - 1, 2) else None,
                        lambda e, a=a, b_=b_, j=j, ct=ct: e.matmul(
                            bank[bk][:], a[:, ct, os_], H8[b_ + ct][:],
                            start=(ct == 0 and j == 0), stop=(ct == NT - 1 and j == 2)))
        zs = Z[:, ot, q * W:(q + 1) * W]
        a = put("act", "yev", lambda e: e.copy(zs, bank[bk][:]), [t, Z_free[ot]])
        bank_free[bk] = [a]
        state["bny"] = put("dve", "bny", lambda e: e.bn_stats(bny[:, ot, 6 * q:6 * q + 6], zs),
                           [a, state.get("bnyfree")])
        state["y", i, q, ot] = a
        for k in range(8):
            H8_free[k] = [t]

    def s_out(i):
        for c1 in range(NT):
            a = put("act", "sev", lambda e, c1=c1: e.copy(XL[c1][:], bank[c1][:]), [state["smm", c1], XL_free[c1]])
            bank_free[c1] = [a]
            XL_free[c1] = []
            state["s", c1] = a

    nx = [0]

    rb_at = {}
    nrb = [0]

    def load_o(b, q, late=False):
        if late:
            k = nrb[0] % NT
            nrb[0] += 1
            place, free, sem = X[:, k, :].rearrange("p (t c) -> p t c", t=4), X_free[k], f"rx{k}"
        else:
            place, free, sem = RB[:], RB_free, "rb"
        rb_at[b, q] = (place, free, dma("sp", sem, place, ot_d[b][q * W:(q + 1) * W, :].rearrange(
            "(t p) c -> p t c", p=P), [free, state["scattered", b]]))

    def load_xr(b, q, tt):
        k = nx[0] % 3
        nx[0] += 1
        state["xr", b, q, tt] = (k, dma("sp", f"xr{k}", XR[k][:], x1_d[b, tt * P:(tt + 1) * P, q * W:(q + 1) * W],
                                        [XR_free[k], state["x1st", b, tt]]))

    def out_unit(b, q, tt, bk):
        place, free, tok = rb_at[b, q]
        wait("pe", bank_free[bk], tok)
        for dt in range(4):
            t = put("pe", "otr" if dt == 3 else None, lambda e, dt=dt: e.transpose(
                bank[bk][:, dt * P:(dt + 1) * P], place[:, dt, tt * P:(tt + 1) * P], ident[:]))
        free[:] = [t]
        if b < B - 1:
            k, tok = state["xr", b, q, tt]
            dst, sem = XR[k][:], f"out{k}"
        else:
            tok, dst, sem = state["x1st", b, tt], Z[:, tt, q * W:(q + 1) * W], f"oz{tt}{q}"
        d = put("dve", "fin", lambda e: e.scalar_tensor_tensor(
            out=dst, in0=bank[bk][:], scalar=bc[:, b, tt:tt + 1], in1=dst, op0=ALU.add, op1=ALU.add),
            [t, tok, state["bc", b]])
        bank_free[bk] = [d]
        st = dma("sp" if b == B - 1 else "pool", sem, out[b, tt * P:(tt + 1) * P, q * W:(q + 1) * W], dst, [d])
        if b < B - 1:
            XR_free[k] = [st]

    def aggr_y(i):
        for ot in range(NT):
            t = put("dve", "mvy", lambda e, ot=ot: e.bn_aggr(mvy[:, ot, :], bny[:, ot, :]),
                    [state["bny"], state.get("mvyfree")])
        state["bnyfree"] = t
        state["mvy"] = put("dve", "mvy", lambda e: e.tensor_copy(am[:, 1, :], mvy[:, :, 0]), [t, state.get("amfree")])

    def v_mm(i, ot):
        bk = ot % 2
        wait("pe", bank_free[bk], S["wp"], *[state["s", c1] for c1 in range(NT)])
        for c1 in range(NT):
            t = put("pe", "vmm" if c1 == NT - 1 else None, lambda e, c1=c1: e.matmul(
                bank[bk][:], WP[:, c1, ot * P:(ot + 1) * P], XL[c1][:], start=(c1 == 0), stop=(c1 == NT - 1)))
        d = put("dve", "att", lambda e: e.tensor_tensor_reduce(
            out=bank[bk][:], in0=bank[bk][:], in1=WG[:, ot, :], scale=1.0, scalar=0.0, op0=ALU.mult, op1=ALU.add,
            accum_out=am[:, 0, ot:ot + 1]), [t, S["wg"], state.get("amfree")])
        bank_free[bk] = [d]
        state["att", ot] = d
        for c1 in range(NT):
            XL_free[c1] = [t]

    def g_mean(i):
        t = put("pe", "gmm", lambda e: e.matmul(
            bank[0][:, 0:8], avg[:], am[:].rearrange("p a b -> p (a b)"), start=True, stop=True),
            [bank_free[0], S["avg"], state["mvy"], *[state["att", o] for o in range(NT)]])
        state["amfree"] = t
        c = put("dve", "gst", lambda e: e.tensor_copy(gm[:].rearrange("p a b -> p (a b)"), bank[0][:, 0:8]),
                [t])
        bank_free[0] = [c]
        d = put("dve", "gst", lambda e: e.tensor_tensor(sm[:, 0, :], am[:, 1, :], gm[:, 1, :], ALU.subtract), [c])
        d = put("dve", "gst", lambda e: e.tensor_tensor(sm[:, 1, :], sm[:, 0, :], sm[:, 0, :], ALU.mult), [d])
        state["sq"] = put("dve", "gst", lambda e: e.tensor_tensor(
            sm[:, 2, :], sm[:, 1, :], mvy[:, :, 1], ALU.add), [d])
        state["mvyfree"] = state["sq"]
        state["att"] = put("dve", "gst", lambda e: e.tensor_scalar(
            sm[:, 3, :], gm[:, 0, :], 64.0, None, ALU.mult), [c])

    def g_var(i):
        t = put("pe", "gmm", lambda e: e.matmul(bank[1][:, 0:4], avg[:], sm[:, 2, :], start=True, stop=True),
                [bank_free[1], state["sq"]])
        d = put("dve", "gst", lambda e: e.tensor_tensor(sm[:, 4, :], bank[1][:, 0:4], sm[:, 3, :], ALU.mult),
                [t, state["att"]])
        bank_free[1] = [d]
        d = put("dve", "gst", lambda e: e.tensor_tensor(sm[:, 4, :], sm[:, 4, :], sm[:, 3, :], ALU.mult), [d])
        p = put("pool", "gpw", lambda e: e.tensor_scalar(ve[:, 2, :], sm[:, 4, :], EPS, None, ALU.add), [d])
        p = put("pool", "gpw", lambda e: e.tensor_tensor(rs[:, 2, :], ve[:, 2, :], half[:], ALU.pow), [p])
        d = put("dve", "gst", lambda e: e.tensor_tensor(sm[:, 0, :], rs[:, 2, :], sm[:, 3, :], ALU.mult), [p])
        d = put("dve", "gst", lambda e: e.tensor_tensor(sm[:, 5, :], sm[:, 0, :], gw[:], ALU.mult),
                [d, S["gw"], state.get("x1")])
        state["A"] = d
        d = put("dve", "gst", lambda e: e.tensor_tensor(sm[:, 1, :], gm[:, 1, :], sm[:, 5, :], ALU.mult), [d])
        state["bc", i] = put("dve", "gst", lambda e: e.tensor_tensor(
            bc[:, i, :], gb[:], sm[:, 1, :], ALU.subtract), [d, S["gb"]])

    def x1_piece(i, ct, q):
        zs, xs = Z[:, ct, q * W:(q + 1) * W], X[:, ct, q * W:(q + 1) * W]
        d = put("dve", "x1", lambda e: e.scalar_tensor_tensor(
            out=zs, in0=zs, scalar=sm[:, 5, ct:ct + 1], in1=xs, op0=ALU.mult, op1=ALU.add),
            [state["A"], state["y", i, q, ct], state["xc", i, q, ct]])
        state["x1"] = d
        X_free[ct] = [d]
        state["x1", i, ct, q] = d

    def bn_x1(i, ct, q):
        state["bn2", ct] = put("dve", "bn2", lambda e: e.bn_stats(
            bn2[:, ct, 6 * q:6 * q + 6], Z[:, ct, q * W:(q + 1) * W]), [state["x1", i, ct, q]])
        if q == NQ - 1:
            t = dma("pool", f"x1_{ct}", x1_d[i, ct * P:(ct + 1) * P, :], Z[:, ct, :], [state["x1", i, ct, q]])
            state["x1st", i, ct] = t
            Z_free[ct] = [t]

    def norm_x1_a(i, ct):
        state["n2", ct] = norm_a("2", ct, bn2, mv2, state["bn2", ct], state.get(("xln2", ct)))

    def norm_x1_b(i, ct):
        state["ln2", i, ct] = norm_b("2", ct, mv2, state["n2", ct])

    nxl, nxt = [0], [0]

    def xln2(i, ct, q):
        k = nxl[0] % NT
        nxl[0] += 1
        t = put("act", "xln2", lambda e: e.activation(
            XL[k][:], Z[:, ct, q * W:(q + 1) * W], ACT.Identity, bias=nm[:, 1, ct:ct + 1],
            scale=rs[:, 1, ct:ct + 1]), [state["ln2", i, ct], state["x1", i, ct, q], XL_free[k]])
        state["xln2", i, ct, q] = (k, t)
        state["xln2", ct] = t

    def turn2(i, ct, q):
        x, tok = state["xln2", i, ct, q]
        bk, k = nxt[0] % 2, nxt[0] % 2
        nxt[0] += 1
        wait("pe", bank_free[bk], tok)
        for dt in range(4):
            t = put("pe", "tr2" if dt == 3 else None, lambda e, dt=dt: e.transpose(
                bank[bk][:, dt * P:(dt + 1) * P], XL[x][:, dt * P:(dt + 1) * P], ident[:]))
        XL_free[x] = [t]
        a = put("act", "xtv", lambda e: e.copy(XT[k][:], bank[bk][:]), [t, XT_free[k]])
        bank_free[bk] = [a]
        XT_free[k] = [dma("sp", f"xt{k}", xg_d[i][q * W:(q + 1) * W, ct * P:(ct + 1) * P].rearrange(
            "(t p) c -> p t c", p=P), XT[k][:].rearrange("p (t c) -> p t c", t=4), [a])]
        if (ct, q) == (NT - 1, NQ - 1):
            state["turned", i] = XT_free[0] + XT_free[1]

    nw, nwl = [0, 0], [0]

    def load_w(h, j):
        src = up[h] if j == 0 else down[h].rearrange("(t p) d -> p t d", p=P)
        dst = WR[:, j, :] if j == 0 else WR[:, j, :].rearrange("p (t d) -> p t d", t=NM)
        state["wr", j] = dma("sp", f"wr{j}", dst, src, WR_free[j])

    def split_w(h, j):
        k = nw[j] % 2
        nw[j] += 1
        a = put("act", "whi", lambda e: e.copy(WH[k][:, j, :], WR[:, j, :]), [state["wr", j], W_free[k][j]])
        d = put("dve", "wlo", lambda e: e.tensor_tensor(WL[k][:, j, :], WR[:, j, :], f(WH[k][:, j, :]),
                                                        ALU.subtract), [a, W_free[k][j]])
        WR_free[j] = [d]
        state["w", k, j] = [a, d]

    ng, ngs = [0], [0]

    def gather(b, h):
        k = ng[0] % 3
        ng[0] += 1
        pl.dma_sems.add(f"gr{k}")
        state["g", b, h] = (k, put("pool", f"gr{k}", lambda e: e.indirect_dma_start(
            out=GR[k][:], out_offset=None, in_=xg_d[b][:, :],
            in_offset=bass.IndirectOffsetOnAxis(ap=perm_sb[:, h:h + 1].bitcast(U32), axis=0)),
            [GR_free[k], state["turned", b], S["perm"]], 16))

    def split_g(b, h):
        k, tok = state["g", b, h]
        s = 2 * (ngs[0] % 4)
        ngs[0] += 1
        a = put("act", "ghi", lambda e: e.copy(T8[s][:], GR[k][:]), [tok, T8_free[s]])
        d = put("dve", "glo", lambda e: e.tensor_tensor(T8[s + 1][:], GR[k][:], f(T8[s][:]), ALU.subtract),
                [a, T8_free[s + 1]])
        GR_free[k] = [d]
        state["gs", b, h] = (s, [a, d])

    nu, nd, na = [0], [0], [0]

    def up_mm(b, h, mt, wk):
        u = nu[0]
        nu[0] += 1
        bk, r, hr = 4 + u % 4, u % 4, u % 3
        s, gtok = state["gs", b, h]
        wait("pe", bank_free[bk], gtok, state["w", wk, 0])
        ms = slice(mt * P, (mt + 1) * P)
        for j, (a, g) in enumerate(((WL[wk], T8[s]), (WH[wk], T8[s + 1]), (WH[wk], T8[s]))):
            t = put("pe", "up" if j == 2 else None, lambda e, a=a, g=g, j=j: e.matmul(
                bank[bk][:], a[:, 0, ms], g[:], start=(j == 0), stop=(j == 2)))
        W_free[wk][0] = [t]
        if mt == NM - 1:
            T8_free[s] = [t]
            T8_free[s + 1] = [t]
        g = put("act", "gelu", lambda e: e.activation(HR[hr][:], bank[bk][:], ACT.Gelu), [t, HR_free[hr]])
        if HI_ACT[u % len(HI_ACT)]:
            hi = put("act", "hhi", lambda e: e.activation(H8[r][:], bank[bk][:], ACT.Gelu), [H8_free[r]])
            bank_free[bk] = [hi]
        else:
            bank_free[bk] = [g]
            hi = put("dve", "hhd", lambda e: e.tensor_copy(H8[r][:], HR[hr][:]), [g, H8_free[r]])
        lo = put("dve", "hlo", lambda e: e.tensor_tensor(H8[4 + r][:], HR[hr][:], f(H8[r][:]), ALU.subtract),
                 [g, hi, H8_free[4 + r]])
        HR_free[hr] = [hi, lo]
        return (b, h, mt, wk, r, [hi, lo])

    def down_mm(b, h, mt, wk, r, htok):
        if mt == 0:
            na[0] += 1
        bk, k = 2 + na[0] % 2, na[0] % 2
        if mt == 0:
            wait("pe", bank_free[bk])
        wait("pe", htok, state["w", wk, 1])
        ms = slice(mt * P, (mt + 1) * P)
        for j, (a, hh) in enumerate(((WL[wk], H8[r]), (WH[wk], H8[4 + r]), (WH[wk], H8[r]))):
            t = put("pe", "dn" if j == 2 else None, lambda e, a=a, hh=hh, j=j: e.matmul(
                bank[bk][:], a[:, 1, ms], hh[:], start=(mt == 0 and j == 0), stop=(mt == NM - 1 and j == 2)))
        H8_free[r] = [t]
        H8_free[4 + r] = [t]
        W_free[wk][1] = [t]
        if mt == NM - 1:
            a = put("act", "oev", lambda e: e.copy(OT[k][:], bank[bk][:]), [t, OT_free[k]])
            bank_free[bk] = [a]
            pl.dma_sems.add(f"sc{k}")
            OT_free[k] = [put("pool", f"sc{k}", lambda e: e.indirect_dma_start(
                out=ot_d[b][:, :], out_offset=bass.IndirectOffsetOnAxis(
                    ap=perm_sb[:, h:h + 1].bitcast(U32), axis=0),
                in_=OT[k][:], in_offset=None), [a, S["perm"]], 16)]
            if h == ND - 1:
                state["scattered", b] = OT_free[0] + OT_free[1]

    HI_ACT = (1, 1, 1, 0)

    def work(i):
        one = lambda b, hs: [(h, [b]) for h in hs]
        two = lambda b, hs: [(h, [b, b + 1]) for h in hs]
        if i == 1:
            return one(0, range(0, 8))
        if i == 2:
            return one(1, range(0, 8)) + two(0, range(8, 12))
        if i == 3:
            return two(0, range(12, 16))
        if 4 <= i < B:
            return two(i // 2 * 2 - 2, range(8 * (i % 2), 8 * (i % 2) + 8))
        if i == B:
            return two(B - 2, range(0, 8)) + one(B - 2, range(8, 16)) + one(B - 1, range(8, 16))
        return []

    def p1_start(i):
        xln(i, 0)
        for ct in range(NT):
            load_c(i, 0, ct)

    def o_load(b, q):
        if 0 <= b < B:
            load_o(b, q)
            for tt in range(3):
                load_xr(b, q, tt)

    def p1(i):
        turn(i, 0)
        b = i - 4
        ws = work(i)
        gs = [(b_, h) for h, bs in ws for b_ in bs]
        if b >= 0:
            o_load(b, 0)
        for q in range(NQ):
            for s in range(4):
                n = 4 * q + s
                if n + 1 < ND:
                    turn(i, n + 1)
                s_mm(i, n)
                if (i, n) == (0, 1):
                    fold()
                if s == 0:
                    for ct in range(NT):
                        split_c(i, q, ct)
                if s == 1:
                    for ct in range(NT):
                        add_c(i, q, ct)
                if s == 2:
                    for ct in range(NT):
                        nxt_q, nxt_i = (q + 1, i) if q + 1 < NQ else (0, i + 1)
                        if not (nxt_i != i and ct >= 2):
                            load_c(nxt_i, nxt_q, ct)
                    if q + 1 < NQ:
                        xln(i, q + 1)
                if b >= 0:
                    for tt in ((), (0, 1), (2,), (3,))[s]:
                        out_unit(b, q, tt, 6 + tt % 2)
                        if tt == 0:
                            load_xr(b, q, 3)
                if s == 3 and b >= 0 and q + 1 < NQ:
                    o_load(b, q + 1)
                if q == NQ - 1 and ws:
                    if s == 0:
                        load_w(ws[0][0], 0)
                        load_w(ws[0][0], 1)
                        gather(*gs[0])
                        gather(*gs[1])
                    if s == 1:
                        split_w(ws[0][0], 0)
                        split_w(ws[0][0], 1)
                    if s == 2:
                        load_w(ws[1][0], 0)
                        load_w(ws[1][0], 1)
                    if s == 3:
                        split_g(*gs[0])
                        gather(*gs[2])
                if n == ND - 1:
                    s_out(i)
                if s >= 2:
                    y_mm(i, q, 2 * (s - 2))
                    y_mm(i, q, 2 * (s - 2) + 1)

    def side_tasks(i):
        r = []
        if i < B:
            r.append((1, lambda: aggr_y(i)))
            for ot in range(NT):
                r.append((2 + 2 * ot, lambda ot=ot: v_mm(i, ot)))
            r.append((10, lambda: g_mean(i)))
            r.append((12, lambda: g_var(i)))
            for ct in range(NT):
                e = 12 + 2.4 * (4 * ct + 3)
                for q in range(NQ):
                    u = 12 + 2.4 * (4 * ct + q)
                    r.append((u, lambda ct=ct, q=q: x1_piece(i, ct, q)))
                    r.append((u + 1, lambda ct=ct, q=q: bn_x1(i, ct, q)))
                    r.append((e + 3.5 + 2 * q, lambda ct=ct, q=q: xln2(i, ct, q)))
                    r.append((e + 5 + 2 * q, lambda ct=ct, q=q: turn2(i, ct, q)))
                    if i + 1 < B:
                        r.append((e + 7 + 2 * q, lambda ct=ct, q=q: bn_x(i + 1, ct, q)))
                if i + 1 < B:
                    r.append((e + 0.5, lambda ct=ct: load_x(i + 1, ct)))
                    r.append((e + 13.8, lambda ct=ct: norm_x_a(i + 1, ct)))
                    r.append((e + 14.8, lambda ct=ct: norm_x_b(i + 1, ct)))
                r.append((e + 1.5, lambda ct=ct: norm_x1_a(i, ct)))
                r.append((e + 2.8, lambda ct=ct: norm_x1_b(i, ct)))
        return r

    def late_tasks():
        r = []

        units = []
        for b, u0, du in ((4, 1, 12), (5, 49, 12), (6, 98.5, 7)):
            for q in range(NQ):
                r.append((u0 + du * q, lambda b=b, q=q: load_o(b, q, True)))
                units += [(u0 + du * (q + tt / 4) + 7, b, q, tt) for tt in range(4)]

        def unit(n):
            if n >= 0:
                out_unit(*units[n][1:], n % 2)
            if n + 3 < len(units):
                load_xr(*units[n + 3][1:])

        r.append((0, lambda: [unit(n) for n in (-3, -2, -1)]))
        for n in range(len(units)):
            r.append((units[n][0], lambda n=n: unit(n)))
        return r

    def fslot(i):
        tasks = sorted(side_tasks(i) if i < B else late_tasks(), key=lambda t: t[0])
        ws = work(i)
        gs = [(b, h) for h, bs in ws for b in bs]
        pend = []
        g = 0
        for w, (h, bs) in enumerate(ws):
            wk = state["wk"]
            state["wk"] = 1 - wk
            for j, b in enumerate(bs):
                for mt in range(NM):
                    u = 4 * g + mt
                    while tasks and tasks[0][0] <= u:
                        tasks.pop(0)[1]()
                    pend.append(up_mm(b, h, mt, wk))
                    if mt == 0:
                        if g + 1 < len(gs):
                            split_g(*gs[g + 1])
                        if g + 3 < len(gs):
                            gather(*gs[g + 3])
                    if len(pend) > LAG:
                        down_mm(*pend.pop(0))
                    if j == 0 and mt in (1, 3) and w + 1 < len(ws):
                        split_w(ws[w + 1][0], mt // 2)
                        if w + 2 < len(ws):
                            load_w(ws[w + 2][0], mt // 2)
                g += 1
        if i == B:
            for a in pend:
                down_mm(*a)
            for _, t in tasks:
                t()
            for q in range(NQ):
                load_o(B - 1, q, True)
            for q in range(NQ):
                for tt in range(4):
                    out_unit(B - 1, q, tt, 4 + (4 * q + tt) % 4)
            return
        for _, t in tasks:
            t()
        if i + 1 < B:
            p1_start(i + 1)
        for a in pend:
            down_mm(*a)

    state["wk"] = 0
    constants()
    for ct in range(NT):
        load_x(0, ct)
    for ct in range(NT):
        load_c(0, 0, ct)
    setup()
    for ct in range(NT):
        for q in range(NQ):
            bn_x(0, ct, q)
        norm_x_a(0, ct)
        norm_x_b(0, ct)
    p1_start(0)
    for i in range(B):
        p1(i)
        fslot(i)
        if i == B - 1:
            ws = work(B)
            gs = [(b, h) for h, bs in ws for b in bs]
            for j in range(2):
                load_w(ws[0][0], j)
            for g in gs[:3]:
                gather(*g)
            for j in range(2):
                split_w(ws[0][0], j)
                load_w(ws[1][0], j)
            split_g(*gs[0])
    fslot(B)

    for name in sorted(pl.dma_sems):
        wait("sp", (name, pl.count[name]))

    block = ctx.enter_context(nc.Block())

    def run(name, eng):
        for fn in pl.queue[name]:
            fn(eng)

    @block.sync
    def _(e):
        run("sp", e)

    @block.tensor
    def _(e):
        run("pe", e)

    @block.scalar
    def _(e):
        run("act", e)

    @block.vector
    def _(e):
        run("dve", e)

    @block.gpsimd
    def _(e):
        run("pool", e)


def kernel(x, ctx_4096, L0_xattn_Wt, L0_xattn_Wp, L0_xattn_Wg, L0_xattn_Wz, L0_xattn_gn_w, L0_xattn_gn_b,
           L0_ffn_up, L0_ffn_down, L0_ffn_perm):
    import numpy as np
    import concourse.bacc as bacc
    from concourse.bass_utils import run_bass_kernel_spmd

    ins = {
        "x": x, "cx": ctx_4096, "Wt": L0_xattn_Wt, "WpT": np.asarray(L0_xattn_Wp).T, "Wg": L0_xattn_Wg,
        "WzT": np.asarray(L0_xattn_Wz).reshape(8, 64, 64).transpose(0, 2, 1),
        "gnw": np.asarray(L0_xattn_gn_w).reshape(4, 128).T, "gnb": np.asarray(L0_xattn_gn_b).reshape(4, 128).T,
        "up": L0_ffn_up, "down": L0_ffn_down, "perm": np.asarray(L0_ffn_perm).reshape(16, 128).T,
    }
    nc = bacc.Bacc("TRN2", target_bir_lowering=False, num_devices=1)
    arrays, args = {}, []
    for name, a in ins.items():
        a = np.ascontiguousarray(a)
        arrays["in_" + name] = a
        args.append(nc.dram_tensor("in_" + name, a.shape, mybir.dt.from_np(a.dtype), kind="ExternalInput").ap())
    args.append(nc.dram_tensor("out_0", (8, 512, 2048), F32, kind="ExternalOutput").ap())
    build(nc, *args)
    r = run_bass_kernel_spmd(nc, [arrays], core_ids=[0])
    return r.results[0]["out_0"]
```

```python
from contextlib import ExitStack

import concourse.bass as bass
from concourse import mybir

F32 = mybir.dt.float32
F32R = mybir.dt.float32r
I32 = mybir.dt.int32
U32 = mybir.dt.uint32
ALU = mybir.AluOpType
ACT = mybir.ActivationFunctionType

B = 8
C = 512
D = 2048
P = 128
NT = C // P
W = 512
NQ = D // W
ND = D // P
M = 512
NM = M // P
EPS = 1e-5
LAG = 4
NC = 6


class Plan:

    def __init__(self, nc, ctx):
        self.nc, self.ctx = nc, ctx
        self.queue = {e: [] for e in ("pe", "act", "dve", "pool", "sp")}
        self.sems, self.count, self.seen = {}, {}, {}
        self.dma_sems = set()

    def sem(self, name):
        if name not in self.sems:
            self.sems[name] = self.ctx.enter_context(self.nc.semaphore("s_" + name))
            self.count[name] = 0
        return self.sems[name]

    def wait(self, e, *tokens):
        for t in tokens:
            if t is None:
                continue
            if isinstance(t, list):
                self.wait(e, *t)
                continue
            name, value = t
            if self.seen.get((e, name), 0) < value:
                self.seen[(e, name)] = value
                self.queue[e].append(lambda eng, s=self.sems[name], v=value: eng.wait_ge(s, v))

    def put(self, e, sem, make, waits=(), by=1):
        self.wait(e, *waits)
        s = self.sem(sem) if sem else None

        def run(eng):
            ins = make(eng)
            if s is not None:
                ins.then_inc(s, by)

        self.queue[e].append(run)
        if sem:
            self.count[sem] += by
            return (sem, self.count[sem])
        return None

    def dma(self, e, sem, out, in_, waits=()):
        self.dma_sems.add(sem)
        return self.put(e, sem, lambda eng: eng.dma_start(out, in_), waits, 16)


def build(nc, x, cx, Wt, WpT, Wg, WzT, gnw, gnb, up, down, perm, out):
    with ExitStack() as ctx:
        build_in(nc, ctx, x, cx, Wt, WpT, Wg, WzT, gnw, gnb, up, down, perm, out)


def build_in(nc, ctx, x, cx, Wt, WpT, Wg, WzT, gnw, gnb, up, down, perm, out):
    def sb(name, shape, dt=F32):
        return ctx.enter_context(nc.sbuf_tensor(name, shape, dt))

    def f(ap):
        return ap.bitcast(F32)

    pl = Plan(nc, ctx)
    put, dma, wait = pl.put, pl.dma, pl.wait

    bank = [ctx.enter_context(nc.psum_tensor(f"bank{k}", [P, 512], F32)) for k in range(8)]

    X = sb("X", [P, NT, D])
    Z = sb("Z", [P, NT, D])
    Ct = [sb(f"C{k}", [P, W]) for k in range(NC)]
    XL = [sb(f"XL{k}", [P, W]) for k in range(NT)]
    H8 = [sb(f"H{k}", [P, 512], F32R) for k in range(8)]
    T8 = [sb(f"T{k}", [P, 512], F32R) for k in range(10)]
    WCH = sb("WCH", [P, NT, C], F32R)
    WCL = sb("WCL", [P, NT, C], F32R)
    WPH = sb("WPH", [P, NT, C], F32R)
    WPL = sb("WPL", [P, NT, C], F32R)
    WW = [[sb(f"W{k}{j}", [P, 2, 512], F32R) for j in range(2)] for k in range(2)]
    GR = [sb(f"GR{k}", [P, 512]) for k in range(3)]
    HR = [sb(f"HR{k}", [P, 512]) for k in range(3)]
    RB = sb("RB", [P, 4, 512])
    XR = [sb(f"XR{k}", [P, W]) for k in range(3)]
    OT = [sb(f"OT{k}", [P, 512]) for k in range(2)]
    XT = [sb(f"XT{k}", [P, 512]) for k in range(2)]
    ident = sb("ident", [P, P])
    avg = sb("avg", [P, P])
    perm_sb = sb("perm_sb", [P, ND], I32)
    gw = sb("gw", [P, NT])
    gb = sb("gb", [P, NT])
    half = sb("half", [P, NT])
    bn1 = sb("bn1", [P, NT, NQ * 6])
    bny = sb("bny", [P, NT, NQ * 6])
    bn2 = sb("bn2", [P, NT, NQ * 6])
    mv1 = sb("mv1", [P, NT, 2])
    mvy = sb("mvy", [P, NT, 2])
    mv2 = sb("mv2", [P, NT, 2])
    ve = sb("ve", [P, 3, NT])
    rs = sb("rs", [P, 3, NT])
    nm = sb("nm", [P, 2, NT])
    am = sb("am", [P, 2, NT])
    gm = sb("gm", [P, 2, NT])
    sm = sb("sm", [P, 6, NT])
    bc = sb("bc", [P, B, NT])


    ot_d = [nc.dram_tensor(f"ot_scratch{b}", [D, C], F32, kind="Internal") for b in range(B)]
    xg_d = [nc.dram_tensor(f"xg_scratch{b}", [D, C], F32, kind="Internal") for b in range(B)]
    w_d = nc.dram_tensor("w_scratch", [ND, 2, P, 2, 512], F32, kind="Internal")
    x1_d = nc.dram_tensor("x1_scratch", [B, C, D], F32, kind="Internal")

    bank_free = [[] for _ in range(8)]
    C_free = [[] for _ in range(NC)]
    XL_free = [[] for _ in range(NT)]
    H8_free = [[] for _ in range(8)]
    T8_free = [[] for _ in range(10)]
    X_free = [[] for _ in range(NT)]
    Z_free = [[] for _ in range(NT)]
    W_free = [[[], []], [[], []]]
    GR_free = [[] for _ in range(3)]
    HR_free = [[] for _ in range(3)]
    RB_free = []
    XR_free = [[] for _ in range(3)]
    OT_free = [[] for _ in range(2)]
    XT_free = [[] for _ in range(2)]

    S = {}

    def setup():
        z = put("dve", "bd0", lambda e: e.memset(Z[:, 0, 1024:1536], 0.0))
        S["wt"] = [dma("sp", "wt", Z[:, :, 0:C], Wt.rearrange("(t p) c -> p t c", p=P))]
        for g in range(2 * NT):
            h = g % 2
            S["wt"].append(dma("sp", f"wz{g}", Z[64 * h:64 * h + 64, 0, 1024 + 64 * g:1088 + 64 * g], WzT[g], [z]))

    def setup_rest():
        S["wp"] = dma("sp", "wp", RB[:], WpT.rearrange("(t p) o -> p t o", p=P))
        S["perm"] = dma("sp", "perm", perm_sb[:], perm)
        S["gw"] = dma("sp", "gw", gw[:], gnw)
        S["gb"] = dma("sp", "gb", gb[:], gnb)

    def constants():
        S["half"] = put("dve", "half", lambda e: e.memset(half[:], -0.5))
        z0 = put("pool", "id0", lambda e: e.memset(ident[:], 0.0))
        S["id"] = put("pool", "id", lambda e: e.affine_select(
            out=ident[:], in_=ident[:], compare_op=ALU.not_equal, fill=1.0, base=0,
            pattern=[[-1, P]], channel_multiplier=1), [z0])
        a0 = put("dve", "avg", lambda e: e.memset(avg[:], 0.0))
        put("dve", "avg", lambda e: e.memset(avg[0:64, 0:64], 1.0 / 64), [a0])
        S["avg"] = put("dve", "avg", lambda e: e.memset(avg[64:128, 64:128], 1.0 / 64))

    def fold():
        wait("pe", S["wt"])
        for ct in range(NT):
            bk = 6 + ct % 2
            wait("pe", bank_free[bk])
            for ot in range(NT):
                pe = put("pe", "wc" if ot == NT - 1 else None, lambda e, bk=bk, ct=ct, ot=ot: e.matmul(
                    bank[bk][:, ot * P:(ot + 1) * P], Z[:, ot, ct * P:(ct + 1) * P],
                    Z[:, 0, 1024 + ot * P:1024 + (ot + 1) * P], start=True, stop=True))
            a = put("act", "wch", lambda e, bk=bk, ct=ct: e.copy(WCH[:, ct, :], bank[bk][:]), [pe])
            S["wc"] = put("dve", "wcl", lambda e, bk=bk, ct=ct: e.tensor_tensor(
                WCL[:, ct, :], bank[bk][:], f(WCH[:, ct, :]), ALU.subtract), [a])
            S["wch"] = a
            bank_free[bk] = [S["wc"]]
        for ct in range(NT):
            Z_free[ct] = [pe]

    state = {}

    def split_wp():
        for c1 in range(NT):
            a = put("act", "wph", lambda e, c1=c1: e.copy(WPH[:, c1, :], RB[:, c1, :]), [S["wp"]])
            S["wps"] = put("dve", "wpl", lambda e, c1=c1: e.tensor_tensor(
                WPL[:, c1, :], RB[:, c1, :], f(WPH[:, c1, :]), ALU.subtract), [a])
        S["wph"] = a
        RB_free[:] = [S["wps"]]

    def load_wg():
        state["wg"] = dma("sp", "wg", RB[:], Wg.rearrange("(t p) o -> p t o", p=P), [RB_free])

    def load_x(i, ct):
        state["x", i, ct] = dma("sp", f"xin{ct}", X[:, ct, :], x[i, ct * P:(ct + 1) * P, :], X_free[ct])

    def bn_x(i, ct, q):
        state["bn1", ct] = put("dve", "bn1", lambda e: e.bn_stats(
            bn1[:, ct, 6 * q:6 * q + 6], X[:, ct, q * W:(q + 1) * W]), [state["x", i, ct]])

    def norm_a(kind, ct, bn, mv, last, free):
        k = {"1": 0, "2": 1}[kind]
        t = put("dve", "mv" + kind, lambda e: e.bn_aggr(mv[:, ct, :], bn[:, ct, :]), [last, free])
        t1 = put("pool", "ve" + kind, lambda e: e.tensor_scalar(
            ve[:, k, ct:ct + 1], mv[:, ct, 1:2], EPS, None, ALU.add), [t])
        return put("pool", "rs" + kind, lambda e: e.tensor_tensor(
            rs[:, k, ct:ct + 1], ve[:, k, ct:ct + 1], half[:, 0:1], ALU.pow), [t1, S["half"]])

    def norm_b(kind, ct, mv, t2):
        k = {"1": 0, "2": 1}[kind]
        t3 = put("dve", "nm" + kind, lambda e: e.scalar_tensor_tensor(
            out=nm[:, k, ct:ct + 1], in0=mv[:, ct, 0:1], scalar=-1.0, in1=rs[:, k, ct:ct + 1],
            op0=ALU.mult, op1=ALU.mult), [t2])
        return [t2, t3]

    def norm_x_a(i, ct):
        state["n1", ct] = norm_a("1", ct, bn1, mv1, state["bn1", ct], state.get(("xln", ct)))

    def norm_x_b(i, ct):
        state["ln1", i, ct] = norm_b("1", ct, mv1, state["n1", ct])

    cslot = {}
    nload = [0]

    def load_c(i, q, ct):
        if (i, q, ct) in cslot or i >= B:
            return
        k = nload[0] % NC
        nload[0] += 1
        cslot[i, q, ct] = k
        state["c", i, q, ct] = dma("sp", f"c{k}", Ct[k][:], cx[i, ct * P:(ct + 1) * P, q * W:(q + 1) * W], C_free[k])
        C_free[k] = []

    def xln(i, q, cts=range(NT)):
        for ct in cts:
            t = put("act", "xln", lambda e, ct=ct: e.activation(
                XL[ct][:], X[:, ct, q * W:(q + 1) * W], ACT.Identity, bias=nm[:, 0, ct:ct + 1],
                scale=rs[:, 0, ct:ct + 1]), [state["x", i, ct], state["ln1", i, ct], XL_free[ct]])
            XL_free[ct] = []
            state["xln", i, q, ct] = t
            state["xln", ct] = t

    def split_c(i, q, ct):
        k = cslot[i, q, ct]
        a = put("act", "chi", lambda e: e.copy(H8[ct][:], Ct[k][:]), [state["c", i, q, ct], H8_free[ct]])
        d = put("dve", "clo", lambda e: e.tensor_tensor(
            H8[4 + ct][:], Ct[k][:], f(H8[ct][:]), ALU.subtract), [a, H8_free[4 + ct]])
        state["cs", i, q, ct] = d
        C_free[k] += [a, d]

    def add_c(i, q, ct):
        k = cslot[i, q, ct]
        xs = X[:, ct, q * W:(q + 1) * W]
        d = put("dve", "xc", lambda e: e.tensor_tensor(xs, xs, Ct[k][:], ALU.add),
                [state["xln", i, q, ct], state["c", i, q, ct], state["bn1", ct]])
        state["xc", i, q, ct] = d
        C_free[k] += [d]

    def turn(i, n):
        q, dt = divmod(n, 4)
        s = 4 * (n % 2)
        b0 = 6 if n == 1 else 4
        pe = []
        for w in range(2):
            bk = b0 + w
            wait("pe", bank_free[bk], S["id"])
            for ct in range(NT):
                k = cslot[i, q, ct]
                src = XL[ct] if w == 0 else Ct[k]
                need = state["xln", i, q, ct] if w == 0 else state["c", i, q, ct]
                t = put("pe", "tr" if ct == NT - 1 else None,
                        lambda e, bk=bk, ct=ct, src=src: e.transpose(
                            bank[bk][:, ct * P:(ct + 1) * P], src[:, dt * P:(dt + 1) * P], ident[:]), [need])
            pe.append(t)
        for ct in range(NT):
            if dt == 3:
                XL_free[ct] = [pe[0]]
                C_free[cslot[i, q, ct]] += [pe[1]]
        for w in range(2):
            h, l, bk = s + 2 * w, s + 2 * w + 1, b0 + w
            a = put("act", "thi", lambda e, h=h, bk=bk: e.copy(T8[h][:], bank[bk][:]), [pe[w], T8_free[h]])
            d = put("dve", "tlo", lambda e, h=h, l=l, bk=bk: e.tensor_tensor(
                T8[l][:], bank[bk][:], f(T8[h][:]), ALU.subtract), [a, T8_free[l]])
            bank_free[bk] = [d]
            state["ts", n, w] = [a, d]

    def s_mm(i, n):
        s = 4 * (n % 2)
        xh, xl, ch, cl = T8[s:s + 4]
        wait("pe", state["ts", n, 0], state["ts", n, 1])
        for c1 in range(NT):
            if n == 0:
                wait("pe", bank_free[c1])
            cs = slice(c1 * P, (c1 + 1) * P)
            for j, (a, b_) in enumerate(((xl, ch), (xh, cl), (xh, ch))):
                t = put("pe", "smm" if j == 2 else None, lambda e, a=a, b_=b_, j=j, c1=c1, cs=cs: e.matmul(
                    bank[c1][:], a[:, cs], b_[:], start=(n == 0 and j == 0), stop=(n == ND - 1 and j == 2)))
            state["smm", c1] = t
        for k in range(s, s + 4):
            T8_free[k] = [t]

    def bn_y(q, ot, tok):
        state["bny"] = put("dve", "bny", lambda e: e.bn_stats(bny[:, ot, 6 * q:6 * q + 6], Z[:, ot, q * W:(q + 1) * W]),
                           [tok, state.get("bnyfree")])

    def y_mm(i, q, ot):
        bk = 6 + ot % 2
        os_ = slice(ot * P, (ot + 1) * P)
        wait("pe", bank_free[bk], S["wc"], S["wch"])
        for ct in range(NT):
            wait("pe", state["cs", i, q, ct])
            for j, (a, b_) in enumerate(((WCL, 0), (WCH, 4), (WCH, 0))):
                t = put("pe", "ymm" if (ct, j) == (NT - 1, 2) else None,
                        lambda e, a=a, b_=b_, j=j, ct=ct: e.matmul(
                            bank[bk][:], a[:, ct, os_], H8[b_ + ct][:],
                            start=(ct == 0 and j == 0), stop=(ct == NT - 1 and j == 2)))
        zs = Z[:, ot, q * W:(q + 1) * W]
        a = put("act", "yev", lambda e: e.copy(zs, bank[bk][:]), [t, Z_free[ot]])
        bank_free[bk] = [a]
        if (i, q) != (0, 0):
            bn_y(q, ot, a)
        state["y", i, q, ot] = a
        for k in range(8):
            H8_free[k] = [t]

    def s_out(i):
        for c1 in range(NT):
            h, l = T8[2 * c1], T8[2 * c1 + 1]
            a = put("act", "sev", lambda e, c1=c1, h=h: e.copy(h[:], bank[c1][:]),
                    [state["smm", c1], T8_free[2 * c1]])
            d = put("dve", "slo", lambda e, c1=c1, h=h, l=l: e.tensor_tensor(
                l[:], bank[c1][:], f(h[:]), ALU.subtract), [a, T8_free[2 * c1 + 1]])
            bank_free[c1] = [d]
            state["s", c1] = [a, d]

    nx = [0]

    rb_at = {}
    nrb = [0]

    def load_o(b, q, late=False):
        if late:
            k = nrb[0] % NT
            nrb[0] += 1
            place, free, sem = X[:, k, :].rearrange("p (t c) -> p t c", t=4), X_free[k], f"rx{k}"
        else:
            place, free, sem = RB[:], RB_free, "rb"
        rb_at[b, q] = (place, free, dma("sp", sem, place, ot_d[b][q * W:(q + 1) * W, :].rearrange(
            "(t p) c -> p t c", p=P), [free, state["scattered", b]]))

    xr_ring = [(XR[k], XR_free, k, f"{k}") for k in range(3)]
    late_ring = [(Ct[k], C_free, k, f"c{k}") for k in range(NC)] + xr_ring

    def load_xr(b, q, tt):
        ring = xr_ring if b < B - 3 else late_ring
        t, free, n, name = ring[nx[0] % len(ring)]
        nx[0] += 1
        state["xr", b, q, tt] = (t, free, n, name, dma(
            "sp", "xr" + name, t[:], x1_d[b, tt * P:(tt + 1) * P, q * W:(q + 1) * W],
            [free[n], state["x1st", b, tt]]))

    def out_unit(b, q, tt, bk):
        place, free, tok = rb_at[b, q]
        wait("pe", bank_free[bk], tok)
        for dt in range(4):
            t = put("pe", "otr" if dt == 3 else None, lambda e, dt=dt: e.transpose(
                bank[bk][:, dt * P:(dt + 1) * P], place[:, dt, tt * P:(tt + 1) * P], ident[:]))
        free[:] = [t]
        if b < B - 1:
            x1, xfree, n, name, tok = state["xr", b, q, tt]
            dst, sem = x1[:], "out" + name
        else:
            tok, dst, sem = state["x1st", b, tt], Z[:, tt, q * W:(q + 1) * W], f"oz{tt}{q}"
        d = put("dve", "fin", lambda e: e.scalar_tensor_tensor(
            out=dst, in0=bank[bk][:], scalar=bc[:, b, tt:tt + 1], in1=dst, op0=ALU.add, op1=ALU.add),
            [t, tok, state["bc", b]])
        bank_free[bk] = [d]
        st = dma("sp" if b == B - 1 else "pool", sem, out[b, tt * P:(tt + 1) * P, q * W:(q + 1) * W], dst, [d])
        if b < B - 1:
            xfree[n] = [st]

    def aggr_y(i):
        for ot in range(NT):
            t = put("dve", "mvy", lambda e, ot=ot: e.bn_aggr(mvy[:, ot, :], bny[:, ot, :]),
                    [state["bny"], state.get("mvyfree")])
        state["bnyfree"] = t
        state["mvy"] = put("dve", "mvy", lambda e: e.tensor_copy(am[:, 1, :], mvy[:, :, 0]), [t, state.get("amfree")])

    def v_mm(i, ot):
        bk = ot % 2
        wait("pe", bank_free[bk], S["wph"], S["wps"], *[state["s", c1] for c1 in range(NT)])
        os_ = slice(ot * P, (ot + 1) * P)
        for c1 in range(NT):
            for j, (a, b_) in enumerate(((WPL, 0), (WPH, 1), (WPH, 0))):
                t = put("pe", "vmm" if (c1, j) == (NT - 1, 2) else None, lambda e, c1=c1, j=j, a=a, b_=b_: e.matmul(
                    bank[bk][:], a[:, c1, os_], T8[2 * c1 + b_][:],
                    start=(c1 == 0 and j == 0), stop=(c1 == NT - 1 and j == 2)))
        d = put("dve", "att", lambda e: e.tensor_tensor_reduce(
            out=bank[bk][:], in0=bank[bk][:], in1=RB[:, ot, :], scale=1.0, scalar=0.0, op0=ALU.mult, op1=ALU.add,
            accum_out=am[:, 0, ot:ot + 1]), [t, state["wg"], state.get("amfree")])
        RB_free[:] = [d]
        late_free[:] = [[d] for _ in range(4)]
        bank_free[bk] = [d]
        state["att", ot] = d
        for k in range(8):
            T8_free[k] = [t]

    def g_mean(i):
        t = put("pe", "gmm", lambda e: e.matmul(
            bank[0][:, 0:8], avg[:], am[:].rearrange("p a b -> p (a b)"), start=True, stop=True),
            [bank_free[0], S["avg"], state["mvy"], *[state["att", o] for o in range(NT)]])
        state["amfree"] = t
        c = put("dve", "gst", lambda e: e.tensor_copy(gm[:].rearrange("p a b -> p (a b)"), bank[0][:, 0:8]),
                [t])
        bank_free[0] = [c]
        d = put("dve", "gst", lambda e: e.tensor_tensor(sm[:, 0, :], am[:, 1, :], gm[:, 1, :], ALU.subtract), [c])
        d = put("dve", "gst", lambda e: e.tensor_tensor(sm[:, 1, :], sm[:, 0, :], sm[:, 0, :], ALU.mult), [d])
        state["sq"] = put("dve", "gst", lambda e: e.tensor_tensor(
            sm[:, 2, :], sm[:, 1, :], mvy[:, :, 1], ALU.add), [d])
        state["mvyfree"] = state["sq"]
        state["att"] = put("dve", "gst", lambda e: e.tensor_scalar(
            sm[:, 3, :], gm[:, 0, :], 64.0, None, ALU.mult), [c])

    def g_var(i):
        t = put("pe", "gmm", lambda e: e.matmul(bank[1][:, 0:4], avg[:], sm[:, 2, :], start=True, stop=True),
                [bank_free[1], state["sq"]])
        d = put("dve", "gst", lambda e: e.tensor_tensor(sm[:, 4, :], bank[1][:, 0:4], sm[:, 3, :], ALU.mult),
                [t, state["att"]])
        bank_free[1] = [d]
        d = put("dve", "gst", lambda e: e.tensor_tensor(sm[:, 4, :], sm[:, 4, :], sm[:, 3, :], ALU.mult), [d])
        p = put("pool", "gpw", lambda e: e.tensor_scalar(ve[:, 2, :], sm[:, 4, :], EPS, None, ALU.add), [d])
        p = put("pool", "gpw", lambda e: e.tensor_tensor(rs[:, 2, :], ve[:, 2, :], half[:], ALU.pow), [p])
        d = put("dve", "gst", lambda e: e.tensor_tensor(sm[:, 0, :], rs[:, 2, :], sm[:, 3, :], ALU.mult), [p])
        d = put("dve", "gst", lambda e: e.tensor_tensor(sm[:, 5, :], sm[:, 0, :], gw[:], ALU.mult),
                [d, S["gw"], state.get("x1")])
        state["A"] = d
        d = put("dve", "gst", lambda e: e.tensor_tensor(sm[:, 1, :], gm[:, 1, :], sm[:, 5, :], ALU.mult), [d])
        state["bc", i] = put("dve", "gst", lambda e: e.tensor_tensor(
            bc[:, i, :], gb[:], sm[:, 1, :], ALU.subtract), [d, S["gb"]])

    def x1_piece(i, ct, q):
        zs, xs = Z[:, ct, q * W:(q + 1) * W], X[:, ct, q * W:(q + 1) * W]
        d = put("dve", "x1", lambda e: e.scalar_tensor_tensor(
            out=zs, in0=zs, scalar=sm[:, 5, ct:ct + 1], in1=xs, op0=ALU.mult, op1=ALU.add),
            [state["A"], state["y", i, q, ct], state["xc", i, q, ct]])
        state["x1"] = d
        X_free[ct] = [d]
        state["x1", i, ct, q] = d

    def bn_x1(i, ct, q):
        state["bn2", ct] = put("dve", "bn2", lambda e: e.bn_stats(
            bn2[:, ct, 6 * q:6 * q + 6], Z[:, ct, q * W:(q + 1) * W]), [state["x1", i, ct, q]])
        if q == NQ - 1:
            t = dma("sp", f"x1_{ct}", x1_d[i, ct * P:(ct + 1) * P, :], Z[:, ct, :], [state["x1", i, ct, q]])
            state["x1st", i, ct] = t
            Z_free[ct] = [t]

    def norm_x1_a(i, ct):
        state["n2", ct] = norm_a("2", ct, bn2, mv2, state["bn2", ct], state.get(("xln2", ct)))

    def norm_x1_b(i, ct):
        state["ln2", i, ct] = norm_b("2", ct, mv2, state["n2", ct])

    nxl, nxp, nxt = [0], [0], [0]

    def xln2(i, ct, q):
        n, tiles, free = (nxl, XL, XL_free) if i == B - 1 else (nxp, OT, OT_free)
        k = n[0] % len(tiles)
        n[0] += 1
        t = put("act", "xln2", lambda e: e.activation(
            tiles[k][:], Z[:, ct, q * W:(q + 1) * W], ACT.Identity, bias=nm[:, 1, ct:ct + 1],
            scale=rs[:, 1, ct:ct + 1]), [state["ln2", i, ct], state["x1", i, ct, q], free[k]])
        free[k] = []
        state["xln2", i, ct, q] = (tiles, free, k, t)
        state["xln2", ct] = t

    def turn2(i, ct, q):
        tiles, free, x, tok = state["xln2", i, ct, q]
        k = nxt[0] % 2
        bk = k if i == B - 1 else 6 + k
        nxt[0] += 1
        wait("pe", bank_free[bk], tok)
        for dt in range(4):
            t = put("pe", "tr2" if dt == 3 else None, lambda e, dt=dt: e.transpose(
                bank[bk][:, dt * P:(dt + 1) * P], tiles[x][:, dt * P:(dt + 1) * P], ident[:]))
        free[x] = [t]
        a = put("act", "xtv", lambda e: e.copy(XT[k][:], bank[bk][:]), [t, XT_free[k]])
        bank_free[bk] = [a]
        XT_free[k] = [dma("sp", f"xt{k}", xg_d[i][q * W:(q + 1) * W, ct * P:(ct + 1) * P].rearrange(
            "(t p) c -> p t c", p=P), XT[k][:].rearrange("p (t c) -> p t c", t=4), [a])]
        if (ct, q) == (NT - 1, NQ - 1):
            state["turned", i] = XT_free[0] + XT_free[1]

    nw = [0, 0]

    early = [((GR[0], GR_free, 0), (GR[1], GR_free, 1)), ((HR[0], HR_free, 0), (HR[1], HR_free, 1))]
    late_free = [[] for _ in range(4)]
    late = [((RB[:, k, :], late_free, k), (RB[:, k + 1, :], late_free, k + 1)) for k in (0, 2)]

    nr = [0, 0]

    def load_raw(h, j, places):
        k = nr[j] % 2
        nr[j] += 1
        t, free, n = places[k][j]
        src = up[h] if j == 0 else down[h].rearrange("(t p) d -> p t d", p=P)
        dst = t[:] if j == 0 else t[:].rearrange("p (t d) -> p t d", t=NM)
        state["wr", h, j] = (t, free, n, dma("sp", f"wr{j}{k}", dst, src, free[n]))

    def split_w(h, j):
        k = nw[j] % 2
        nw[j] += 1
        w = WW[k][j]
        t, free, n, tok = state["wr", h, j]
        a = put("act", "whi", lambda e: e.copy(w[:, 0, :], t[:]), [tok, W_free[k][j]])
        d = put("dve", "wlo", lambda e: e.tensor_tensor(w[:, 1, :], t[:], f(w[:, 0, :]),
                                                        ALU.subtract), [a, W_free[k][j]])
        free[n] = [d]
        state["w", k, j] = [a, d]

    def keep_w(h, j):
        k = h % 2
        W_free[k][j] = [dma("sp", f"ws{j}{k}", w_d[h, j], f(WW[k][j][:]), [state["w", k, j]])]
        state["wd", h, j] = W_free[k][j]

    def load_w(h, j):
        k = nw[j] % 2
        nw[j] += 1
        state["w", k, j] = dma("act", f"w{j}{k}", f(WW[k][j][:]), w_d[h, j], [W_free[k][j], state["wd", h, j]])

    ng, ngs = [0], [0]

    def gather(b, h):
        k = ng[0] % 3
        ng[0] += 1
        pl.dma_sems.add(f"gr{k}")
        state["g", b, h] = (k, put("pool", f"gr{k}", lambda e: e.indirect_dma_start(
            out=GR[k][:], out_offset=None, in_=xg_d[b][:, :],
            in_offset=bass.IndirectOffsetOnAxis(ap=perm_sb[:, h:h + 1].bitcast(U32), axis=0)),
            [GR_free[k], state["turned", b], S["perm"]], 16))

    def split_g(b, h):
        k, tok = state["g", b, h]
        s = 2 * (ngs[0] % 5)
        ngs[0] += 1
        a = put("act", "ghi", lambda e: e.copy(T8[s][:], GR[k][:]), [tok, T8_free[s]])
        d = put("dve", "glo", lambda e: e.tensor_tensor(T8[s + 1][:], GR[k][:], f(T8[s][:]), ALU.subtract),
                [a, T8_free[s + 1]])
        GR_free[k] = [d]
        state["gs", b, h] = (s, [a, d])

    nu, na, done = [0], [0], [0] * B

    def up_mm(b, h, mt, wk):
        u = nu[0]
        nu[0] += 1
        bk, r, hr = 4 + u % 4, u % 4, u % 3
        s, gtok = state["gs", b, h]
        wait("pe", bank_free[bk], gtok, state["w", wk, 0])
        ms = slice(mt * P, (mt + 1) * P)
        for j, (a, g) in enumerate(((1, T8[s]), (0, T8[s + 1]), (0, T8[s]))):
            t = put("pe", "up" if j == 2 else None, lambda e, a=a, g=g, j=j: e.matmul(
                bank[bk][:], WW[wk][0][:, a, ms], g[:], start=(j == 0), stop=(j == 2)))
        W_free[wk][0] = [t]
        if mt == NM - 1:
            T8_free[s] = [t]
            T8_free[s + 1] = [t]
        return (b, h, mt, wk, u, bk, r, hr, t)

    def hidden(b, h, mt, wk, u, bk, r, hr, t):
        g = put("act", "gelu", lambda e: e.activation(HR[hr][:], bank[bk][:], ACT.Gelu), [t, HR_free[hr]])
        hi = put("act", "hhi", lambda e: e.activation(H8[r][:], bank[bk][:], ACT.Gelu), [H8_free[r]])
        bank_free[bk] = [hi]
        lo = put("dve", "hlo", lambda e: e.tensor_tensor(H8[4 + r][:], HR[hr][:], f(H8[r][:]), ALU.subtract),
                 [g, hi, H8_free[4 + r]])
        HR_free[hr] = [hi, lo]
        return (b, h, mt, wk, r, [hi, lo])

    def down_mm(b, h, mt, wk, r, htok):
        if mt == 0:
            na[0] += 1
        bk, k = 2 + na[0] % 2, na[0] % 2
        if mt == 0:
            wait("pe", bank_free[bk])
        wait("pe", htok, state["w", wk, 1])
        ms = slice(mt * P, (mt + 1) * P)
        for j, (a, hh) in enumerate(((1, H8[r]), (0, H8[4 + r]), (0, H8[r]))):
            t = put("pe", "dn" if j == 2 else None, lambda e, a=a, hh=hh, j=j: e.matmul(
                bank[bk][:], WW[wk][1][:, a, ms], hh[:], start=(mt == 0 and j == 0), stop=(mt == NM - 1 and j == 2)))
        H8_free[r] = [t]
        H8_free[4 + r] = [t]
        W_free[wk][1] = [t]
        return (b, h, mt, k, bk, t)

    def down_out(b, h, mt, k, bk, t):
        if mt == NM - 1:
            a = put("act", "oev", lambda e: e.copy(OT[k][:], bank[bk][:]), [t, OT_free[k]])
            bank_free[bk] = [a]
            pl.dma_sems.add(f"sc{k}")
            OT_free[k] = [put("pool", f"sc{k}", lambda e: e.indirect_dma_start(
                out=ot_d[b][:, :], out_offset=bass.IndirectOffsetOnAxis(
                    ap=perm_sb[:, h:h + 1].bitcast(U32), axis=0),
                in_=OT[k][:], in_offset=None), [a, S["perm"]], 16)]
            done[b] += 1
            if done[b] == ND:
                state["scattered", b] = OT_free[0] + OT_free[1]

    def work(i):
        if i == 0:
            return []
        half = [8 * (i % 2) + h for h in range(8)]
        if i == 1:
            return [(h, [0]) for h in half]
        if i < B:
            return [(h, [i - 2, i - 1]) for h in half]
        rest = [h for h in range(ND) if h not in half[4:]]
        return [(h, [B - 2]) for h in half[:4]] + [(h, [B - 2, B - 1]) for h in half[4:]] + [(h, [B - 1]) for h in rest]

    def o_load(b, q):
        if 0 <= b < B:
            load_o(b, q)
            for tt in range(3):
                load_xr(b, q, tt)

    def p3_in_p1(i, q, s):
        if i < 0:
            return
        if q == 0:
            for ct in tail_tiles(i):
                if s == (1 if i < 2 and ct > 1 else 0):
                    tail_stats(i, ct)
        steps = lambda q: ((0, 1), (2, 3), (), ()) if q else ((), (), (0, 1), (2, 3))
        for ct in steps(q)[s]:
            turn2(i, ct, q)
        nq, nz = (q, s + 1) if s < 3 else (q + 1, 0)
        if nq < NQ:
            for ct in steps(nq)[nz]:
                xln2(i, ct, nq)

    def tail_tiles(i):
        return () if i == B - 1 else (NT - 1,) if i > 1 else range(NT) if i == 0 else range(1, NT)

    def tail_stats(i, ct):
        for q in range(NQ):
            bn_x1(i, ct, q)
        norm_x1_a(i, ct)
        norm_x1_b(i, ct)

    def p1(i):
        turn(i, 0)
        b = i - 3
        ws = work(i)
        gs = [(b_, h) for h, bs in ws for b_ in bs]
        if b >= 0:
            o_load(b, 0)
        for q in range(NQ):
            for s in range(4):
                n = 4 * q + s
                if n + 1 < ND:
                    turn(i, n + 1)
                p3_in_p1(i - 1, q, s)
                s_mm(i, n)
                if (i, n) == (0, 6):
                    split_wp()
                if s == 2 and i in (1, 2) and q == 0:
                    for ct in range(NT):
                        add_c(i, q, ct)
                if s == 2:
                    for ct in range(NT):
                        nxt_q, nxt_i = (q + 1, i) if q + 1 < NQ else (0, i + 1)
                        if not (nxt_i != i and ct >= 2):
                            load_c(nxt_i, nxt_q, ct)
                    if q + 1 < NQ:
                        xln(i, q + 1)
                    if b >= 0:
                        load_xr(b, q, 3)
                if i == 0:
                    for j in range(2):
                        if n > 0:
                            keep_w(n - 1, j)
                        split_w(n, j)
                        if n + 2 < ND:
                            load_raw(n + 2, j, early)
                if b >= 0:
                    for tt in ((), (0, 1), (2,), (3,))[s]:
                        out_unit(b, q, tt, 6 if tt == 0 else 7)
                if s == (0 if q or i < 3 else 1) and (i, q) != (0, 0):
                    for ct in range(NT):
                        split_c(i, q, ct)
                if s == 1 and not (i in (1, 2) and q == 0):
                    for ct in range(NT):
                        add_c(i, q, ct)
                if s == 3 and b >= 0 and q + 1 < NQ:
                    o_load(b, q + 1)
                if ws and q == NQ - 1 and s < 2:
                    for j in range(2):
                        load_w(ws[s][0], j)
                if ws and q == NQ - 1:
                    if s == (0 if i > 1 else 2):
                        gather(*gs[0])
                    if s == 2:
                        gather(*gs[1])
                    if s == 3:
                        ngs[0] = 4
                        split_g(*gs[0])
                        gather(*gs[2])
                if n == ND - 1:
                    if i == 0:
                        for j in range(2):
                            keep_w(n, j)
                    s_out(i)
                    load_wg()
                if s >= 2 and (i, q) != (0, 0):
                    y_mm(i, q, 2 * (s - 2))
                    y_mm(i, q, 2 * (s - 2) + 1)

    def side_tasks(i):
        last = i == B - 1
        gs, base, span = {0: (4, 8, 16), 1: (1.5, 5.5, 24), B - 1: (1.5, 5, 40)}.get(i, (1.5, 5.5, 48))
        sp = span / 16
        r = [(-1, lambda: aggr_y(i))]
        for ot in range(NT):
            r.append((0, lambda ot=ot: v_mm(i, ot)))
        r.append((gs, lambda: g_mean(i)))
        r.append((gs + 3, lambda: g_var(i)))
        for ct in range(NT):
            e = base + sp * (4 * ct + 3)
            n = e + 5 if i else base + 16 + 4 * ct
            d = min(sp, 2.2)
            for q in range(NQ):
                u = base + sp * (4 * ct + q)
                r.append((u, lambda ct=ct, q=q: x1_piece(i, ct, q)))
                if ct not in tail_tiles(i):
                    r.append((u + 1.3, lambda ct=ct, q=q: bn_x1(i, ct, q)))
                if last:
                    r.append((e + 4 + 2 * q, lambda ct=ct, q=q: xln2(i, ct, q)))
                    r.append((e + 7.3 + 2 * q, lambda ct=ct, q=q: turn2(i, ct, q)))
                else:
                    r.append((n + d * q, lambda ct=ct, q=q: bn_x(i + 1, ct, q)))
            if not last:
                r.append((e + 0.5, lambda ct=ct: load_x(i + 1, ct)))
                r.append((n + 3 * d + 0.8, lambda ct=ct: norm_x_a(i + 1, ct)))
                r.append((n + 3 * d + 1.8, lambda ct=ct: norm_x_b(i + 1, ct)))
                r.append((n + 3 * d + 3.5, lambda ct=ct: xln(i + 1, 0, [ct])))
                r.append((n + 3 * d + 2.6, lambda ct=ct: load_c(i + 1, 0, ct)))
            if ct not in tail_tiles(i):
                r.append((e + 1.6, lambda ct=ct: norm_x1_a(i, ct)))
                r.append((e + 3.1, lambda ct=ct: norm_x1_b(i, ct)))
        return r

    def late_tasks():
        r = []

        units = []
        for b, u0, du in ((B - 3, 65, 11), (B - 2, 116, 9)):
            for q in range(NQ):
                r.append((u0 + du * q, lambda b=b, q=q: load_o(b, q, True)))
                units += [(u0 + du * (q + tt / 4) + 7, b, q, tt) for tt in range(4)]

        def unit(n):
            if n >= 0:
                out_unit(*units[n][1:], n % 2)
            if n + 6 < len(units):
                load_xr(*units[n + 6][1:])

        r.append((65, lambda: [unit(n) for n in range(-6, 0)]))
        for n in range(len(units)):
            r.append((units[n][0], lambda n=n: unit(n)))
        return r

    def fslot(i):
        last = i == B - 1
        tasks = sorted(side_tasks(i) + (late_tasks() if last else []), key=lambda t: t[0])
        ws = work(i) + (work(B) if last else [])
        nk = len(work(i))
        gs = [(b, h) for h, bs in ws for b in bs]
        pend = []
        g = 0
        for w, (h, bs) in enumerate(ws):
            wk = state["wk"]
            state["wk"] = 1 - wk
            for j, b in enumerate(bs):
                for mt in range(NM):
                    u = 4 * g + mt
                    while tasks and tasks[0][0] <= u:
                        tasks.pop(0)[1]()
                    if g and mt == 0 and g + 1 < len(gs):
                        split_g(*gs[g + 1])
                    a = up_mm(b, h, mt, wk)
                    d = down_mm(*pend.pop(0)) if len(pend) >= LAG else None
                    more = j == 0 and mt in (0, 3) and 1 <= w < nk - 1
                    if more and i == 1:
                        load_w(ws[w + 1][0], mt // 3)
                    pend.append(hidden(*a))
                    if more and i > 1:
                        load_w(ws[w + 1][0], mt // 3)
                    if d:
                        down_out(*d)
                    if (g, mt) == (0, 0):
                        split_g(*gs[1])
                    if mt == 0 and g + 3 < len(gs):
                        gather(*gs[g + 3])
                    if j == 0 and mt in (1, 3):
                        if nk <= w + 1 < len(ws):
                            split_w(ws[w + 1][0], mt // 2)
                        if nk <= w + 3 < len(ws):
                            load_raw(ws[w + 3][0], mt // 2, late)
                g += 1
        if last:
            for a in pend:
                down_out(*down_mm(*a))
            for _, t in tasks:
                t()
            for q in range(NQ):
                load_o(B - 1, q, True)
            for q in range(NQ):
                for tt in range(4):
                    out_unit(B - 1, q, tt, 4 + (4 * q + tt) % 4)
            return
        for _, t in tasks:
            t()
        for a in pend:
            down_out(*down_mm(*a))

    state["wk"] = 0
    constants()
    setup()
    for ct in range(NT):
        load_c(0, 0, ct)
    for ct in range(NT):
        load_x(0, ct)
    setup_rest()
    for h in range(2):
        for j in range(2):
            load_raw(h, j, early)
    fold()
    for ct in range(NT):
        split_c(0, 0, ct)
    for ot in range(NT):
        y_mm(0, 0, ot)
    for ct in range(NT):
        for q in range(NQ):
            bn_x(0, ct, q)
            if q == 1 and ct > 0:
                norm_x_b(0, ct - 1)
        norm_x_a(0, ct)
    norm_x_b(0, NT - 1)
    xln(0, 0)
    for ot in range(NT):
        bn_y(0, ot, state["y", 0, 0, ot])
    for i in range(B):
        p1(i)
        fslot(i)

    for name in sorted(pl.dma_sems):
        wait("sp", (name, pl.count[name]))

    block = ctx.enter_context(nc.Block())

    def run(name, eng):
        for fn in pl.queue[name]:
            fn(eng)

    @block.sync
    def _(e):
        run("sp", e)

    @block.tensor
    def _(e):
        run("pe", e)

    @block.scalar
    def _(e):
        run("act", e)

    @block.vector
    def _(e):
        run("dve", e)

    @block.gpsimd
    def _(e):
        run("pool", e)


def kernel(x, ctx_4096, L0_xattn_Wt, L0_xattn_Wp, L0_xattn_Wg, L0_xattn_Wz, L0_xattn_gn_w, L0_xattn_gn_b,
           L0_ffn_up, L0_ffn_down, L0_ffn_perm):
    import numpy as np
    import concourse.bacc as bacc
    from concourse.bass_utils import run_bass_kernel_spmd

    ins = {
        "x": x, "cx": ctx_4096, "Wt": L0_xattn_Wt, "WpT": np.asarray(L0_xattn_Wp).T, "Wg": L0_xattn_Wg,
        "WzT": np.asarray(L0_xattn_Wz).reshape(8, 64, 64).transpose(0, 2, 1),
        "gnw": np.asarray(L0_xattn_gn_w).reshape(4, 128).T, "gnb": np.asarray(L0_xattn_gn_b).reshape(4, 128).T,
        "up": L0_ffn_up, "down": L0_ffn_down, "perm": np.asarray(L0_ffn_perm).reshape(16, 128).T,
    }
    nc = bacc.Bacc("TRN2", target_bir_lowering=False, num_devices=1)
    arrays, args = {}, []
    for name, a in ins.items():
        a = np.ascontiguousarray(a)
        arrays["in_" + name] = a
        args.append(nc.dram_tensor("in_" + name, a.shape, mybir.dt.from_np(a.dtype), kind="ExternalInput").ap())
    args.append(nc.dram_tensor("out_0", (8, 512, 2048), F32, kind="ExternalOutput").ap())
    build(nc, *args)
    r = run_bass_kernel_spmd(nc, [arrays], core_ids=[0])
    return r.results[0]["out_0"]
```
